# Optimizing a Trainium2 kernel written in Bass

```python
import numpy as np
import jax
import jax.numpy as jnp

def _softmax(x, axis=-1):
    return jax.nn.softmax(x, axis=axis)

def _gelu(x):
    return jax.nn.gelu(x, approximate=True)

def _silu(x):
    return jax.nn.silu(x)

def _sigmoid(x):
    return jax.nn.sigmoid(x)

def _layernorm(x, axis=-1, eps=1e-05):
    m = jnp.mean(x, axis=axis, keepdims=True)
    v = jnp.var(x, axis=axis, keepdims=True)
    return (x - m) / jnp.sqrt(v + eps)

def _scatter_add(tgt, idx, src, axis=0):
    return tgt.at[idx].add(src)

def _segment_sum(src, seg, n):
    return jax.ops.segment_sum(src, seg, n)
kernel_name = 'mk_adj_preln_d2_adj_r2_b6896c'

def setup_inputs(seed: int=0):
    np.random.seed(seed)
    _w = jnp.asarray

    def _rec_inputs():
        import jax
        import jax.numpy as jnp
        _gk = jax.random.key(seed)
        x = -0.000929 + 1 * jax.random.normal(jax.random.fold_in(_gk, 1), (4096, 128), jnp.float32)
        _a = jax.random.bernoulli(jax.random.fold_in(_gk, 2), 0.000976562, (4096, 4096))
        _af = _a.astype(jnp.float32)
        adj = _af
        return (x, adj)
    x, adj = _rec_inputs()

    def _L0_gnn_setup():
        import jax, jax.numpy as jnp
        import numpy as np
        N, IN_DIM, OUT_DIM, HEADS = (2048, 128, 128, 4)
        D_K = OUT_DIM // HEADS
        NEG_SLOPE = 0.2
        key = jax.random.key(seed)
        k1, k2, k3, k4, k5 = jax.random.split(key, 5)
        H = jax.random.normal(k1, (N, IN_DIM), dtype=jnp.float32)
        A = jax.random.randint(k2, (N, N), 0, 2).astype(jnp.float32)
        W = jax.random.normal(k3, (OUT_DIM, IN_DIM), dtype=jnp.float32) * (1.0 / np.sqrt(IN_DIM))
        a_l = jax.random.normal(k4, (HEADS, D_K), dtype=jnp.float32) * 0.1
        a_r = jax.random.normal(k5, (HEADS, D_K), dtype=jnp.float32) * 0.1
        return {'H': H, 'A': A, 'W': W, 'a_l': a_l, 'a_r': a_r}
    _L0_gnn_all = _L0_gnn_setup()
    _L0_gnn_in = {k: v for k, v in _L0_gnn_all.items() if k in ('W', 'a_l', 'a_r')}
    del _L0_gnn_all

    def _L1_gnn_setup():
        import jax, jax.numpy as jnp
        import numpy as np
        N, IN_FEAT, OUT_FEAT, H = (2048, 128, 128, 8)
        D = OUT_FEAT // H
        ADJ_DENSITY = 0.05
        key = jax.random.key(seed)
        kx, kw, kb, ka, kadj = jax.random.split(key, 5)
        x = jax.random.normal(kx, (N, IN_FEAT), dtype=jnp.float32)
        W = jax.random.normal(kw, (OUT_FEAT, IN_FEAT), dtype=jnp.float32) * (1.0 / np.sqrt(IN_FEAT))
        b = jax.random.normal(kb, (OUT_FEAT,), dtype=jnp.float32) * 0.01
        a = jax.random.normal(ka, (H, 2 * D), dtype=jnp.float32)
        adj_matrix = jax.random.bernoulli(kadj, ADJ_DENSITY, (N, N)).astype(jnp.float32)
        return {'x': x, 'W': W, 'b': b, 'a': a, 'adj_matrix': adj_matrix}
    _L1_gnn_all = _L1_gnn_setup()
    _L1_gnn_in = {k: v for k, v in _L1_gnn_all.items() if k in ('W', 'b', 'a')}
    del _L1_gnn_all
    return {'x': x, 'adj': adj, 'L0_gnn_W': _L0_gnn_in['W'], 'L0_gnn_a_l': _L0_gnn_in['a_l'], 'L0_gnn_a_r': _L0_gnn_in['a_r'], 'L1_gnn_W': _L1_gnn_in['W'], 'L1_gnn_b': _L1_gnn_in['b'], 'L1_gnn_a': _L1_gnn_in['a']}

def reference(x, adj, L0_gnn_W, L0_gnn_a_l, L0_gnn_a_r, L1_gnn_W, L1_gnn_b, L1_gnn_a):
    import jax
    import jax.numpy as jnp

    def _L0_gnn_ref(H, A, W, a_l, a_r):
        import jax, jax.numpy as jnp
        import numpy as np
        N, IN_DIM, OUT_DIM, HEADS = (2048, 128, 128, 4)
        D_K = OUT_DIM // HEADS
        NEG_SLOPE = 0.2
        n = H.shape[0]
        A_tilde = A + jnp.eye(n, dtype=A.dtype)
        mask = A_tilde > 0
        Wh = (H @ W.T).reshape(n, HEADS, D_K)
        score_l = jnp.einsum('nhd,hd->nh', Wh, a_l)
        score_r = jnp.einsum('nhd,hd->nh', Wh, a_r)
        e = score_l[:, :, None] + score_r.T[None, :, :]
        e = jnp.where(e >= 0, e, NEG_SLOPE * e)
        e = jnp.where(mask[:, None, :], e, -jnp.inf)
        alpha = jax.nn.softmax(e, axis=2)
        out = jnp.einsum('nhm,mhd->nhd', alpha, Wh).reshape(n, OUT_DIM)
        return jax.nn.elu(out)

    def _L1_gnn_ref(x, W, b, a, adj_matrix):
        import jax, jax.numpy as jnp
        import numpy as np
        N, IN_FEAT, OUT_FEAT, H = (2048, 128, 128, 8)
        D = OUT_FEAT // H
        ADJ_DENSITY = 0.05
        num_nodes = x.shape[0]
        num_heads = a.shape[0]
        half = a.shape[1] // 2
        node_feats = (x @ W.T + b).reshape(num_nodes, num_heads, half)
        logit_parent = (node_feats * a[None, :, :half]).sum(axis=-1)
        logit_child = (node_feats * a[None, :, half:]).sum(axis=-1)
        attn_logits = logit_parent[:, None, :] + logit_child[None, :, :]
        attn_logits = jax.nn.leaky_relu(attn_logits, 0.2)
        attn_logits = jnp.where(jnp.abs(adj_matrix)[..., None] != 0.0, attn_logits, 0.0)
        attn_probs = jax.nn.softmax(attn_logits, axis=1)
        out = jnp.einsum('ijh,jhc->ihc', attn_probs, node_feats)
        return out.reshape(num_nodes, -1)
    h = jnp.maximum(_layernorm(x, axis=-1), 0.0)
    x = x + _L0_gnn_ref(h, adj, L0_gnn_W, L0_gnn_a_l, L0_gnn_a_r)
    h = jnp.maximum(_layernorm(x, axis=-1), 0.0)
    x = x + _L1_gnn_ref(h, L1_gnn_W, L1_gnn_b, L1_gnn_a, adj)
    return x

_drawn_inputs = setup_inputs


def setup_inputs(seed=0):
    import zlib

    import numpy as np

    out = dict(_drawn_inputs(seed))
    spreads = {}
    factors = {'L0_gnn_a_l': 3.053, 'L1_gnn_b': 6.495}
    for name, (base, spread) in spreads.items():
        noise = np.random.default_rng([zlib.crc32(name.encode()), seed]).standard_normal(out[name].shape)
        drawn = base * np.exp(spread * noise) if base else spread * noise
        out[name] = jnp.asarray(drawn.astype(out[name].dtype))
    for name, factor in factors.items():
        out[name] = (out[name] * factor).astype(out[name].dtype)
    return out
```

```python
from contextlib import ExitStack

import concourse.bass as bass
from concourse import mybir

F32 = mybir.dt.float32
U32 = mybir.dt.uint32
I32 = mybir.dt.int32
BF16 = mybir.dt.bfloat16
ALU = mybir.AluOpType
ACT = mybir.ActivationFunctionType
AX_X = mybir.AxisListType.X

P = 128
N = 4096
D = 128
T = N // P
H0, H1 = 4, 8
D0, D1 = D // H0, D // H1
S0, S1 = D + 4 * H0, D + 4 * H1
SM = S1
SLOPE = 0.2
EPS = 1e-5
BIG = 1e30
CHUNK = 512
NCH = N // CHUNK
BPC = CHUNK // P


class Memory:
    pass


def allocate(nc, ctx):
    m = Memory()

    def sb(name, shape, dt=F32):
        return ctx.enter_context(nc.sbuf_tensor(name, shape, dt))

    m.ident = sb("ident", [P, P])
    m.ones = sb("ones", [P, P])
    m.head0 = sb("head0", [P, H0])
    m.head1 = sb("head1", [P, H1])
    m.w_in = sb("w_in", [P, 2, D])
    m.a_in = sb("a_in", [P, 5])
    m.spread0 = sb("spread0", [P, 4 * H0])
    m.spread1 = sb("spread1", [P, 4 * H1])
    m.weights0 = sb("weights0", [P, S0])
    m.weights1 = sb("weights1", [P, S1])
    m.bias_row = sb("bias_row", [1, S1])
    m.eps = sb("eps", [P, 1])
    m.x_sb = sb("x_sb", [P, T, D])
    m.table = sb("table", [P, T, SM])
    m.stats = sb("stats", [P, T, 6])
    m.mean_var = sb("mean_var", [P, T, 2])
    m.rstd = sb("rstd", [P, T])
    m.normed = sb("normed", [P, 2, D])
    m.h_t = sb("h_t", [P, 2, P])
    m.psum = [ctx.enter_context(nc.psum_tensor(f"bank{b}", [P, CHUNK], F32)) for b in range(8)]
    return m


def prepare(nc, ctx, m, W0, al, ar, W1, b1, a1):
    def sem(name):
        return ctx.enter_context(nc.semaphore(name))

    w_loaded, shapes, folded, on_pe, evacuated = (
        sem("w_loaded"), sem("shapes"), sem("folded"), sem("on_pe"), sem("evacuated"))

    with nc.Block() as block:
        @block.sync
        def _(sp):
            sp.dma_start(m.w_in[:, 0, :], W0[:, :]).then_inc(w_loaded, 16)
            sp.dma_start(m.w_in[:, 1, :], W1[:, :]).then_inc(w_loaded, 16)
            sp.dma_start(m.a_in[:, 0:1], ar.rearrange("h (d o) -> (h d) o", o=1)).then_inc(w_loaded, 16)
            sp.dma_start(m.a_in[:, 1:2], al.rearrange("h (d o) -> (h d) o", o=1)).then_inc(w_loaded, 16)
            sp.dma_start(m.a_in[:, 4:5], b1.rearrange("(d o) -> d o", o=1)).then_inc(w_loaded, 16)
            for half, col in ((1, 2), (0, 3)):
                for h in range(H1):
                    sp.dma_start(m.a_in[h * D1:(h + 1) * D1, col:col + 1],
                                 a1[h, half * D1:(half + 1) * D1].rearrange("(d o) -> d o", o=1)).then_inc(w_loaded, 16)

        @block.gpsimd
        def _(pool):
            pool.memset(m.ident[:, :], 0.0).then_inc(shapes, 1)
            pool.memset(m.ones[:, :], 1.0).then_inc(shapes, 1)
            pool.memset(m.head0[:, :], 1.0).then_inc(shapes, 1)
            pool.memset(m.head1[:, :], 1.0).then_inc(shapes, 1)
            pool.memset(m.eps[:, :], EPS).then_inc(shapes, 1)
            pool.wait_ge(shapes, 5)
            pool.affine_select(out=m.ident[:, :], in_=m.ident[:, :], compare_op=ALU.not_equal, fill=1.0,
                               base=0, pattern=[[-1, P]], channel_multiplier=1).then_inc(shapes, 1)
            for mask, heads, d in ((m.head0, H0, D0), (m.head1, H1, D1)):
                pool.affine_select(out=mask[:, :], in_=mask[:, :], compare_op=ALU.is_ge, fill=0.0,
                                   base=0, pattern=[[-d, heads]], channel_multiplier=1).then_inc(shapes, 1)
            pool.wait_ge(shapes, 8)
            for mask, heads, d in ((m.head0, H0, D0), (m.head1, H1, D1)):
                pool.affine_select(out=mask[:, :], in_=mask[:, :], compare_op=ALU.is_ge, fill=0.0,
                                   base=d - 1, pattern=[[d, heads]], channel_multiplier=-1).then_inc(shapes, 1)

        @block.vector
        def _(dve):
            dve.wait_ge(w_loaded, (5 + 2 * H1) * 16)
            dve.wait_ge(shapes, 10)
            for k in range(2):
                dve.tensor_scalar(m.spread0[:, 2 * k * H0:(2 * k + 1) * H0], m.head0[:, :], m.a_in[:, k:k + 1], None,
                                  ALU.mult).then_inc(folded, 1)
                dve.tensor_scalar(m.spread1[:, 2 * k * H1:(2 * k + 1) * H1], m.head1[:, :], m.a_in[:, 2 + k:3 + k],
                                  None, ALU.mult).then_inc(folded, 1)
            dve.wait_ge(folded, 4)
            for k in range(2):
                for sp_, h in ((m.spread0, H0), (m.spread1, H1)):
                    dve.tensor_scalar(sp_[:, (2 * k + 1) * h:(2 * k + 2) * h], sp_[:, 2 * k * h:(2 * k + 1) * h],
                                      SLOPE, None, ALU.mult).then_inc(folded, 1)
            dve.wait_ge(on_pe, 6)
            dve.tensor_copy(m.weights0[:, 0:D], m.psum[0][:, 0:D]).then_inc(evacuated, 1)
            dve.tensor_copy(m.weights1[:, 0:D], m.psum[1][:, 0:D]).then_inc(evacuated, 1)
            dve.tensor_copy(m.weights0[:, D:S0], m.psum[2][:, 0:4 * H0]).then_inc(evacuated, 1)
            dve.tensor_copy(m.weights1[:, D:S1], m.psum[3][:, 0:4 * H1]).then_inc(evacuated, 1)
            dve.tensor_copy(m.bias_row[:, 0:D], m.psum[4][0:1, 0:D]).then_inc(evacuated, 1)
            dve.tensor_copy(m.bias_row[:, D:S1], m.psum[5][0:1, 0:4 * H1]).then_inc(evacuated, 1)
            dve.wait_ge(evacuated, 6)

        @block.tensor
        def _(pe):
            pe.wait_ge(w_loaded, (5 + 2 * H1) * 16)
            pe.wait_ge(shapes, 10)
            pe.transpose(m.psum[0][:, 0:D], m.w_in[:, 0, :], m.ident[:, :]).then_inc(on_pe, 1)
            pe.transpose(m.psum[1][:, 0:D], m.w_in[:, 1, :], m.ident[:, :]).then_inc(on_pe, 1)
            pe.wait_ge(folded, 8)
            pe.matmul(m.psum[2][:, 0:4 * H0], m.w_in[:, 0, :], m.spread0[:, :], start=True, stop=True).then_inc(on_pe, 1)
            pe.matmul(m.psum[3][:, 0:4 * H1], m.w_in[:, 1, :], m.spread1[:, :], start=True, stop=True).then_inc(on_pe, 1)
            pe.matmul(m.psum[4][0:1, 0:D], m.a_in[:, 4:5], m.ident[:, :], start=True, stop=True).then_inc(on_pe, 1)
            pe.matmul(m.psum[5][0:1, 0:4 * H1], m.a_in[:, 4:5], m.spread1[:, :], start=True, stop=True).then_inc(on_pe, 1)


def load_x(nc, ctx, m, x, tag):
    x_loaded = ctx.enter_context(nc.semaphore("x_loaded" + tag))
    with nc.Block() as block:
        @block.sync
        def _(sp):
            sp.dma_start(m.x_sb[:, :, :], x.rearrange("(t p) d -> p t d", p=P)).then_inc(x_loaded, 16)
            sp.wait_ge(x_loaded, 16)


def transform(nc, ctx, m, layer, tag):
    weights, cols = (m.weights0, S0) if layer == 0 else (m.weights1, S1)

    def sem(name):
        return ctx.enter_context(nc.semaphore(name + tag))

    stats_done, var_done, root_done, rstd_done, norm_done, turned, relu_done, product_done, stored = (
        sem("stats_done"), sem("var_done"), sem("root_done"), sem("rstd_done"), sem("norm_done"), sem("turned"),
        sem("relu_done"), sem("product_done"), sem("stored"))

    with nc.Block() as block:
        @block.vector
        def _(dve):
            with dve.Fori(0, T) as t:
                dve.bn_stats(m.stats[:, bass.ds(t, 1), :], m.x_sb[:, bass.ds(t, 1), :]).then_inc(stats_done, 1)
            dve.wait_ge(stats_done, T)
            for t in range(T):
                dve.bn_aggr(m.mean_var[:, t, :], m.stats[:, t, :]).then_inc(var_done, 1)
            dve.wait_ge(root_done, 1)
            dve.reciprocal(m.rstd[:, :], m.rstd[:, :]).then_inc(rstd_done, 1)
            dve.wait_ge(rstd_done, 1)

            def norm(t, b):
                dve.tensor_scalar(m.normed[:, b, :], m.x_sb[:, bass.ds(t, 1), :], m.mean_var[:, bass.ds(t, 1), 0:1],
                                  m.rstd[:, bass.ds(t, 1)], ALU.subtract, ALU.mult).then_inc(norm_done, 1)
            for b in range(2):
                norm(b, b)
            with dve.Fori(1, T // 2) as i:
                for b in range(2):
                    dve.wait_ge(turned, 2 * i + b - 1)
                    norm(2 * i + b, b)

        @block.scalar
        def _(act):
            act.wait_ge(var_done, T)
            act.activation(m.rstd[:, :], m.mean_var[:, :, 1], ACT.Sqrt, bias=m.eps[:, 0:1]).then_inc(root_done, 1)

            def relu(t, b):
                act.wait_ge(turned, t + 1)
                act.activation(m.h_t[:, b, :], m.psum[b][:, 0:P], ACT.Relu).then_inc(relu_done, 1)

            def store(t, b):
                act.wait_ge(product_done, t + 1)
                act.activation(m.table[:, bass.ds(t, 1), 0:cols], m.psum[2 + b][:, 0:cols], ACT.Copy).then_inc(stored, 1)
            relu(0, 0)
            relu(1, 1)
            store(0, 0)
            with act.Fori(1, T // 2) as i:
                relu(2 * i, 0)
                store(2 * i - 1, 1)
                relu(2 * i + 1, 1)
                store(2 * i, 0)
            store(T - 1, 1)

        @block.tensor
        def _(pe):
            def turn(t, b):
                pe.wait_ge(norm_done, t + 1)
                pe.transpose(m.psum[b][:, 0:P], m.normed[:, b, :], m.ident[:, :]).then_inc(turned, 1)

            def product(t, b):
                pe.wait_ge(relu_done, t + 1)
                last = pe.matmul(m.psum[2 + b][:, 0:cols], m.h_t[:, b, :], weights[:, :], start=True,
                                 stop=layer == 0)
                if layer == 1:
                    last = pe.matmul(m.psum[2 + b][:, 0:cols], m.ones[0:1, :], m.bias_row[:, :], start=False, stop=True)
                last.then_inc(product_done, 1)
            turn(0, 0)
            turn(1, 1)
            product(0, 0)
            with pe.Fori(1, T // 2) as i:
                turn(2 * i, 0)
                product(2 * i - 1, 1)
                turn(2 * i + 1, 1)
                pe.wait_ge(stored, 2 * i - 1)
                product(2 * i, 0)
            product(T - 1, 1)


def attend_any(nc, ctx, m, layer, adj, g, tag):
    heads, dh = (H0, D0) if layer == 0 else (H1, D1)

    def sem(name):
        return ctx.enter_context(nc.semaphore(name + tag))

    diag_done, spread_done, row_done, a_loaded, chain, shifted, exp_done, turned, turn_copied, summed, normed = (
        sem("diag_done"), sem("spread_done"), sem("row_done"), sem("a_loaded"), sem("chain"), sem("shifted"),
        sem("exp_done"), sem("turned"), sem("turn_copied"), sem("summed"), sem("normed"))
    STEPS = 7 if layer == 0 else 5

    with nc.Block() as block:
        @block.sync
        def _(sp):
            sp.dma_start(g.adj[:, :], adj[0:P, :]).then_inc(a_loaded, 16)
            with sp.Fori(1, heads * T) as k:
                sp.wait_ge(shifted, k)
                sp.dma_start(g.adj[:, :], adj[bass.ds((k % T) * P, P), :]).then_inc(a_loaded, 16)

        @block.vector
        def _(dve):
            with dve.Fori(0, heads) as h:
                for c in range(NCH):
                    if c:
                        dve.wait_ge(spread_done, h * NCH + c)
                    dve.tensor_tensor(g.diag[:, :, :], m.ident[:, None, :].to_broadcast([P, BPC, P]),
                                      m.table[:, c * BPC:(c + 1) * BPC, bass.ds(D + h, 1)].to_broadcast([P, BPC, P]),
                                      ALU.mult).then_inc(diag_done, 1)
                with dve.Fori(0, T) as i:
                    k = h * T + i
                    at = [0]

                    def step(ins):
                        ins.then_inc(chain, 1)
                        at[0] += 1
                        dve.wait_ge(chain, k * STEPS + at[0])
                    dve.wait_ge(a_loaded, 16 * k + 16)
                    if layer == 0:
                        here = g.adj[:, bass.ds(i * P, P)]
                        step(dve.tensor_tensor(here, here, m.ident[:, :], ALU.add))
                    step(dve.tensor_scalar(g.adj[:, :], g.adj[:, :], 0.0, None,
                                           ALU.is_gt if layer == 0 else ALU.not_equal))
                    dve.wait_ge(row_done, h * NCH + NCH)
                    step(dve.tensor_scalar(g.e[:, :], g.row[:, :],
                                           m.table[:, bass.ds(i, 1), bass.ds(D + 2 * heads + h, 1)], None, ALU.add))
                    step(dve.scalar_tensor_tensor(out=g.e[:, :], in0=g.e[:, :], scalar=SLOPE, in1=g.e[:, :],
                                                  op0=ALU.mult, op1=ALU.max))
                    if layer == 0:
                        step(dve.tensor_scalar(g.adj[:, :], g.adj[:, :], BIG, -BIG, ALU.mult, ALU.add))
                        step(dve.tensor_tensor(g.e[:, :], g.e[:, :], g.adj[:, :], ALU.add))
                    else:
                        step(dve.tensor_tensor(g.e[:, :], g.e[:, :], g.adj[:, :], ALU.mult))
                    step(dve.reduce_max(g.top[:, 0:1], g.e[:, :], AX_X))
                    dve.tensor_scalar(g.top[:, 1:2], g.top[:, 0:1], -1.0, None, ALU.mult).then_inc(shifted, 1)
                    for c in range(NCH):
                        dve.wait_ge(turned, k * NCH + c + 1)
                        if c >= 2:
                            dve.wait_ge(summed, k * NCH + c - 1)
                        dve.tensor_copy(g.p_t[:, c % 2, :], m.psum[c % 2][:, :]).then_inc(turn_copied, 1)
                    dve.wait_ge(summed, k * NCH + NCH)
                    dve.reciprocal(g.top[:, 3:4], g.top[:, 2:3]).then_inc(normed, 1)
                    dve.wait_ge(normed, 2 * k + 1)
                    dve.tensor_scalar(g.att[:, bass.ds(i, 1), bass.ds(h * dh, dh)], m.psum[3][:, 0:dh],
                                      g.top[:, 3:4], None, ALU.mult).then_inc(normed, 1)
                    dve.wait_ge(normed, 2 * k + 2)

        @block.scalar
        def _(act):
            with act.Fori(0, heads) as h:
                for c in range(NCH):
                    act.wait_ge(spread_done, h * NCH + c + 1)
                    act.activation(g.row[:, c * CHUNK:(c + 1) * CHUNK], m.psum[2][:, :], ACT.Copy).then_inc(row_done, 1)
                with act.Fori(0, T) as i:
                    k = h * T + i
                    act.wait_ge(shifted, k + 1)
                    act.activation(g.e[:, :], g.e[:, :], ACT.Exp, bias=g.top[:, 1:2],
                                   accum_out=g.top[:, 2:3]).then_inc(exp_done, 1)

        @block.tensor
        def _(pe):
            with pe.Fori(0, heads) as h:
                for c in range(NCH):
                    pe.wait_ge(diag_done, h * NCH + c + 1)
                    if c:
                        pe.wait_ge(row_done, h * NCH + c)
                    pe.matmul(m.psum[2][:, :], m.ones[:, :], g.diag[:, :, :], start=True, stop=True).then_inc(spread_done, 1)
                with pe.Fori(0, T) as i:
                    k = h * T + i

                    def turn(c):
                        if c >= 2:
                            pe.wait_ge(turn_copied, k * NCH + c - 1)
                        for b in range(BPC):
                            last = pe.transpose(m.psum[c % 2][:, b * P:(b + 1) * P],
                                                g.e[:, c * CHUNK + b * P:c * CHUNK + (b + 1) * P], m.ident[:, :])
                        last.then_inc(turned, 1)
                    pe.wait_ge(exp_done, k + 1)
                    turn(0)
                    for c in range(NCH):
                        if c + 1 < NCH:
                            turn(c + 1)
                        pe.wait_ge(turn_copied, k * NCH + c + 1)
                        for b in range(BPC):
                            blk = c * BPC + b
                            last = pe.matmul(m.psum[3][:, 0:dh], g.p_t[:, c % 2, b * P:(b + 1) * P],
                                             m.table[:, blk, bass.ds(h * dh, dh)], start=blk == 0, stop=blk == T - 1)
                        last.then_inc(summed, 1)


def finish_any(nc, ctx, m, layer, out, g, tag):
    def sem(name):
        return ctx.enter_context(nc.semaphore(name + tag))

    low, exp_done, high, added, written = sem("low"), sem("exp_done"), sem("high"), sem("added"), sem("written")
    flat = g.att[:, :, :].rearrange("p t d -> p (t d)")
    x_flat = m.x_sb[:, :, :].rearrange("p t d -> p (t d)")
    with nc.Block() as block:
        @block.vector
        def _(dve):
            if layer == 0:
                dve.tensor_scalar(g.e[:, :], flat, 0.0, None, ALU.min).then_inc(low, 1)
                dve.tensor_scalar(flat, flat, 0.0, -1.0, ALU.max, ALU.add).then_inc(high, 1)
                dve.wait_ge(high, 1)
                dve.wait_ge(exp_done, 1)
                dve.tensor_tensor(flat, flat, g.e[:, :], ALU.add).then_inc(high, 1)
                dve.wait_ge(high, 2)
            dve.tensor_tensor(x_flat, x_flat, flat, ALU.add).then_inc(added, 1)

        @block.scalar
        def _(act):
            if layer == 0:
                act.wait_ge(low, 1)
                act.activation(g.e[:, :], g.e[:, :], ACT.Exp).then_inc(exp_done, 1)

        @block.sync
        def _(sp):
            if layer == 1:
                sp.wait_ge(added, 1)
                sp.dma_start(out.rearrange("(t p) d -> p t d", p=P), m.x_sb[:, :, :]).then_inc(written, 16)
                sp.wait_ge(written, 16)


def any_path(nc, ctx, m, x, adj, out):
    def sb(name, shape, dt=F32):
        return ctx.enter_context(nc.sbuf_tensor(name, shape, dt))

    g = Memory()
    g.adj = sb("any_adj", [P, N])
    g.e = sb("any_e", [P, N])
    g.row = sb("any_row", [P, N])
    g.att = sb("any_att", [P, T, D])
    g.diag = sb("any_diag", [P, BPC, P])
    g.p_t = sb("any_p_t", [P, 2, CHUNK])
    g.top = sb("any_top", [P, 4])
    load_x(nc, ctx, m, x, "_any")
    for layer in range(2):
        transform(nc, ctx, m, layer, f"_nodes{layer}")
        attend_any(nc, ctx, m, layer, adj, g, f"_any{layer}")
        finish_any(nc, ctx, m, layer, out, g, f"_end{layer}")


def build(nc, x, adj, W0, al, ar, W1, b1, a1, out):
    with ExitStack() as ctx:
        m = allocate(nc, ctx)
        prepare(nc, ctx, m, W0, al, ar, W1, b1, a1)
        any_path(nc, ctx, m, x, adj, out)


_INS = ['x', 'adj', 'L0_gnn_W', 'L0_gnn_a_l', 'L0_gnn_a_r', 'L1_gnn_W', 'L1_gnn_b', 'L1_gnn_a']
_OUTS = [((4096, 128), 'float32')]


def kernel(**inputs):
    import numpy as _np
    import concourse.bacc as _bacc
    from concourse import mybir as _mybir
    from concourse.bass_utils import run_bass_kernel_spmd as _run
    nc = _bacc.Bacc("TRN2", target_bir_lowering=False, num_devices=1)
    arrays, args = {}, []
    for name in _INS:
        a = _np.ascontiguousarray(inputs[name])
        arrays[f"in_{name}_dram"] = a
        args.append(nc.dram_tensor(f"in_{name}_dram", a.shape, _mybir.dt.from_np(a.dtype), kind="ExternalInput").ap())
    for i, (shape, dtype) in enumerate(_OUTS):
        dt = _mybir.dt.from_np(_np.dtype(dtype))
        args.append(nc.dram_tensor(f"out_{i}_dram", shape, dt, kind="ExternalOutput").ap())
    build(nc, *args)
    r = _run(nc, [arrays], core_ids=[0])
    return r.results[0]["out_0_dram"]
```

```python
from contextlib import ExitStack

import concourse.bass as bass
from concourse import mybir

F32 = mybir.dt.float32
U32 = mybir.dt.uint32
I32 = mybir.dt.int32
BF16 = mybir.dt.bfloat16
ALU = mybir.AluOpType
ACT = mybir.ActivationFunctionType
AX_X = mybir.AxisListType.X

P = 128
N = 4096
D = 128
T = N // P
H0, H1 = 4, 8
D0, D1 = D // H0, D // H1
S0, S1 = D + 4 * H0, D + 4 * H1
SM = S1
SLOPE = 0.2
EPS = 1e-5
BIG = 1e30
CHUNK = 512
NCH = N // CHUNK
BPC = CHUNK // P

SEG = 1024
NSEG = N // SEG
FOUND = 8
CAND = NSEG * FOUND
K = 16
EC = 5
E = EC * P
G0, G1 = D + 2 * H0, D + 2 * H1
V0, V1 = D + H0, D + H1
HIT = float(N)
DEN_MAX = 1e30


class Memory:
    pass


def allocate(nc, ctx):
    m = Memory()

    def sb(name, shape, dt=F32):
        return ctx.enter_context(nc.sbuf_tensor(name, shape, dt))

    m.ident = sb("ident", [P, P])
    m.ones = sb("ones", [P, P])
    m.head0 = sb("head0", [P, H0])
    m.head1 = sb("head1", [P, H1])
    m.w_in = sb("w_in", [P, 2, D])
    m.a_in = sb("a_in", [P, 5])
    m.spread0 = sb("spread0", [P, 4 * H0])
    m.spread1 = sb("spread1", [P, 4 * H1])
    m.weights0 = sb("weights0", [P, S0])
    m.weights1 = sb("weights1", [P, S1])
    m.bias_row = sb("bias_row", [1, S1])
    m.eps = sb("eps", [P, 1])
    m.x_sb = sb("x_sb", [P, T, D])
    m.table = sb("table", [P, T, SM])
    m.stats = sb("stats", [P, T, 6])
    m.mean_var = sb("mean_var", [P, T, 2])
    m.rstd = sb("rstd", [P, T])
    m.normed = sb("normed", [P, 2, D])
    m.h_t = sb("h_t", [P, 2, P])
    m.psum_all = ctx.enter_context(nc.psum_tensor("psum_all", [P, 8 * CHUNK], F32))
    m.psum = [m.psum_all[:, b * CHUNK:(b + 1) * CHUNK] for b in range(8)]
    return m


def prepare(nc, ctx, m, W0, al, ar, W1, b1, a1):
    def sem(name):
        return ctx.enter_context(nc.semaphore(name))

    w_loaded, shapes, folded, on_pe, evacuated = (
        sem("w_loaded"), sem("shapes"), sem("folded"), sem("on_pe"), sem("evacuated"))

    with nc.Block() as block:
        @block.sync
        def _(sp):
            sp.dma_start(m.w_in[:, 0, :], W0[:, :]).then_inc(w_loaded, 16)
            sp.dma_start(m.w_in[:, 1, :], W1[:, :]).then_inc(w_loaded, 16)
            sp.dma_start(m.a_in[:, 0:1], ar.rearrange("h (d o) -> (h d) o", o=1)).then_inc(w_loaded, 16)
            sp.dma_start(m.a_in[:, 1:2], al.rearrange("h (d o) -> (h d) o", o=1)).then_inc(w_loaded, 16)
            sp.dma_start(m.a_in[:, 4:5], b1.rearrange("(d o) -> d o", o=1)).then_inc(w_loaded, 16)
            for half, col in ((1, 2), (0, 3)):
                for h in range(H1):
                    sp.dma_start(m.a_in[h * D1:(h + 1) * D1, col:col + 1],
                                 a1[h, half * D1:(half + 1) * D1].rearrange("(d o) -> d o", o=1)).then_inc(w_loaded, 16)

        @block.gpsimd
        def _(pool):
            pool.memset(m.ident[:, :], 0.0).then_inc(shapes, 1)
            pool.memset(m.ones[:, :], 1.0).then_inc(shapes, 1)
            pool.memset(m.head0[:, :], 1.0).then_inc(shapes, 1)
            pool.memset(m.head1[:, :], 1.0).then_inc(shapes, 1)
            pool.memset(m.eps[:, :], EPS).then_inc(shapes, 1)
            pool.wait_ge(shapes, 5)
            pool.affine_select(out=m.ident[:, :], in_=m.ident[:, :], compare_op=ALU.not_equal, fill=1.0,
                               base=0, pattern=[[-1, P]], channel_multiplier=1).then_inc(shapes, 1)
            for mask, heads, d in ((m.head0, H0, D0), (m.head1, H1, D1)):
                pool.affine_select(out=mask[:, :], in_=mask[:, :], compare_op=ALU.is_ge, fill=0.0,
                                   base=0, pattern=[[-d, heads]], channel_multiplier=1).then_inc(shapes, 1)
            pool.wait_ge(shapes, 8)
            for mask, heads, d in ((m.head0, H0, D0), (m.head1, H1, D1)):
                pool.affine_select(out=mask[:, :], in_=mask[:, :], compare_op=ALU.is_ge, fill=0.0,
                                   base=d - 1, pattern=[[d, heads]], channel_multiplier=-1).then_inc(shapes, 1)

        @block.vector
        def _(dve):
            dve.wait_ge(w_loaded, (5 + 2 * H1) * 16)
            dve.wait_ge(shapes, 10)
            for k in range(2):
                dve.tensor_scalar(m.spread0[:, 2 * k * H0:(2 * k + 1) * H0], m.head0[:, :], m.a_in[:, k:k + 1], None,
                                  ALU.mult).then_inc(folded, 1)
                dve.tensor_scalar(m.spread1[:, 2 * k * H1:(2 * k + 1) * H1], m.head1[:, :], m.a_in[:, 2 + k:3 + k],
                                  None, ALU.mult).then_inc(folded, 1)
            dve.wait_ge(folded, 4)
            for k in range(2):
                for sp_, h in ((m.spread0, H0), (m.spread1, H1)):
                    dve.tensor_scalar(sp_[:, (2 * k + 1) * h:(2 * k + 2) * h], sp_[:, 2 * k * h:(2 * k + 1) * h],
                                      SLOPE, None, ALU.mult).then_inc(folded, 1)
            dve.wait_ge(on_pe, 6)
            dve.tensor_copy(m.weights0[:, 0:D], m.psum[0][:, 0:D]).then_inc(evacuated, 1)
            dve.tensor_copy(m.weights1[:, 0:D], m.psum[1][:, 0:D]).then_inc(evacuated, 1)
            dve.tensor_copy(m.weights0[:, D:S0], m.psum[2][:, 0:4 * H0]).then_inc(evacuated, 1)
            dve.tensor_copy(m.weights1[:, D:S1], m.psum[3][:, 0:4 * H1]).then_inc(evacuated, 1)
            dve.tensor_copy(m.bias_row[:, 0:D], m.psum[4][0:1, 0:D]).then_inc(evacuated, 1)
            dve.tensor_copy(m.bias_row[:, D:S1], m.psum[5][0:1, 0:4 * H1]).then_inc(evacuated, 1)
            dve.wait_ge(evacuated, 6)

        @block.tensor
        def _(pe):
            pe.wait_ge(w_loaded, (5 + 2 * H1) * 16)
            pe.wait_ge(shapes, 10)
            pe.transpose(m.psum[0][:, 0:D], m.w_in[:, 0, :], m.ident[:, :]).then_inc(on_pe, 1)
            pe.transpose(m.psum[1][:, 0:D], m.w_in[:, 1, :], m.ident[:, :]).then_inc(on_pe, 1)
            pe.wait_ge(folded, 8)
            pe.matmul(m.psum[2][:, 0:4 * H0], m.w_in[:, 0, :], m.spread0[:, :], start=True, stop=True).then_inc(on_pe, 1)
            pe.matmul(m.psum[3][:, 0:4 * H1], m.w_in[:, 1, :], m.spread1[:, :], start=True, stop=True).then_inc(on_pe, 1)
            pe.matmul(m.psum[4][0:1, 0:D], m.a_in[:, 4:5], m.ident[:, :], start=True, stop=True).then_inc(on_pe, 1)
            pe.matmul(m.psum[5][0:1, 0:4 * H1], m.a_in[:, 4:5], m.spread1[:, :], start=True, stop=True).then_inc(on_pe, 1)


def load_x(nc, ctx, m, x, tag):
    x_loaded = ctx.enter_context(nc.semaphore("x_loaded" + tag))
    with nc.Block() as block:
        @block.sync
        def _(sp):
            sp.dma_start(m.x_sb[:, :, :], x.rearrange("(t p) d -> p t d", p=P)).then_inc(x_loaded, 16)
            sp.wait_ge(x_loaded, 16)


def transform(nc, ctx, m, layer, tag):
    weights, cols = (m.weights0, S0) if layer == 0 else (m.weights1, S1)

    def sem(name):
        return ctx.enter_context(nc.semaphore(name + tag))

    stats_done, var_done, root_done, rstd_done, norm_done, turned, relu_done, product_done, stored = (
        sem("stats_done"), sem("var_done"), sem("root_done"), sem("rstd_done"), sem("norm_done"), sem("turned"),
        sem("relu_done"), sem("product_done"), sem("stored"))

    with nc.Block() as block:
        @block.vector
        def _(dve):
            with dve.Fori(0, T) as t:
                dve.bn_stats(m.stats[:, bass.ds(t, 1), :], m.x_sb[:, bass.ds(t, 1), :]).then_inc(stats_done, 1)
            dve.wait_ge(stats_done, T)
            for t in range(T):
                dve.bn_aggr(m.mean_var[:, t, :], m.stats[:, t, :]).then_inc(var_done, 1)
            dve.wait_ge(root_done, 1)
            dve.reciprocal(m.rstd[:, :], m.rstd[:, :]).then_inc(rstd_done, 1)
            dve.wait_ge(rstd_done, 1)

            def norm(t, b):
                dve.tensor_scalar(m.normed[:, b, :], m.x_sb[:, bass.ds(t, 1), :], m.mean_var[:, bass.ds(t, 1), 0:1],
                                  m.rstd[:, bass.ds(t, 1)], ALU.subtract, ALU.mult).then_inc(norm_done, 1)
            for b in range(2):
                norm(b, b)
            with dve.Fori(1, T // 2) as i:
                for b in range(2):
                    dve.wait_ge(turned, 2 * i + b - 1)
                    norm(2 * i + b, b)

        @block.scalar
        def _(act):
            act.wait_ge(var_done, T)
            act.activation(m.rstd[:, :], m.mean_var[:, :, 1], ACT.Sqrt, bias=m.eps[:, 0:1]).then_inc(root_done, 1)

            def relu(t, b):
                act.wait_ge(turned, t + 1)
                act.activation(m.h_t[:, b, :], m.psum[b][:, 0:P], ACT.Relu).then_inc(relu_done, 1)

            def store(t, b):
                act.wait_ge(product_done, t + 1)
                act.activation(m.table[:, bass.ds(t, 1), 0:cols], m.psum[2 + b][:, 0:cols], ACT.Copy).then_inc(stored, 1)
            relu(0, 0)
            relu(1, 1)
            store(0, 0)
            with act.Fori(1, T // 2) as i:
                relu(2 * i, 0)
                store(2 * i - 1, 1)
                relu(2 * i + 1, 1)
                store(2 * i, 0)
            store(T - 1, 1)

        @block.tensor
        def _(pe):
            def turn(t, b):
                pe.wait_ge(norm_done, t + 1)
                pe.transpose(m.psum[b][:, 0:P], m.normed[:, b, :], m.ident[:, :]).then_inc(turned, 1)

            def product(t, b):
                pe.wait_ge(relu_done, t + 1)
                last = pe.matmul(m.psum[2 + b][:, 0:cols], m.h_t[:, b, :], weights[:, :], start=True,
                                 stop=layer == 0)
                if layer == 1:
                    last = pe.matmul(m.psum[2 + b][:, 0:cols], m.ones[0:1, :], m.bias_row[:, :], start=False, stop=True)
                last.then_inc(product_done, 1)
            turn(0, 0)
            turn(1, 1)
            product(0, 0)
            with pe.Fori(1, T // 2) as i:
                turn(2 * i, 0)
                product(2 * i - 1, 1)
                turn(2 * i + 1, 1)
                pe.wait_ge(stored, 2 * i - 1)
                product(2 * i, 0)
            product(T - 1, 1)


def attend_any(nc, ctx, m, layer, adj, g, tag):
    heads, dh = (H0, D0) if layer == 0 else (H1, D1)

    def sem(name):
        return ctx.enter_context(nc.semaphore(name + tag))

    diag_done, spread_done, row_done, a_loaded, chain, shifted, exp_done, turned, turn_copied, summed, normed = (
        sem("diag_done"), sem("spread_done"), sem("row_done"), sem("a_loaded"), sem("chain"), sem("shifted"),
        sem("exp_done"), sem("turned"), sem("turn_copied"), sem("summed"), sem("normed"))
    STEPS = 7 if layer == 0 else 5

    with nc.Block() as block:
        @block.sync
        def _(sp):
            sp.dma_start(g.adj[:, :], adj[0:P, :]).then_inc(a_loaded, 16)
            with sp.Fori(1, heads * T) as k:
                sp.wait_ge(shifted, k)
                sp.dma_start(g.adj[:, :], adj[bass.ds((k % T) * P, P), :]).then_inc(a_loaded, 16)

        @block.vector
        def _(dve):
            with dve.Fori(0, heads) as h:
                for c in range(NCH):
                    if c:
                        dve.wait_ge(spread_done, h * NCH + c)
                    dve.tensor_tensor(g.diag[:, :, :], m.ident[:, None, :].to_broadcast([P, BPC, P]),
                                      m.table[:, c * BPC:(c + 1) * BPC, bass.ds(D + h, 1)].to_broadcast([P, BPC, P]),
                                      ALU.mult).then_inc(diag_done, 1)
                with dve.Fori(0, T) as i:
                    k = h * T + i
                    at = [0]

                    def step(ins):
                        ins.then_inc(chain, 1)
                        at[0] += 1
                        dve.wait_ge(chain, k * STEPS + at[0])
                    dve.wait_ge(a_loaded, 16 * k + 16)
                    if layer == 0:
                        here = g.adj[:, bass.ds(i * P, P)]
                        step(dve.tensor_tensor(here, here, m.ident[:, :], ALU.add))
                    step(dve.tensor_scalar(g.adj[:, :], g.adj[:, :], 0.0, None,
                                           ALU.is_gt if layer == 0 else ALU.not_equal))
                    dve.wait_ge(row_done, h * NCH + NCH)
                    step(dve.tensor_scalar(g.e[:, :], g.row[:, :],
                                           m.table[:, bass.ds(i, 1), bass.ds(D + 2 * heads + h, 1)], None, ALU.add))
                    step(dve.scalar_tensor_tensor(out=g.e[:, :], in0=g.e[:, :], scalar=SLOPE, in1=g.e[:, :],
                                                  op0=ALU.mult, op1=ALU.max))
                    if layer == 0:
                        step(dve.tensor_scalar(g.adj[:, :], g.adj[:, :], BIG, -BIG, ALU.mult, ALU.add))
                        step(dve.tensor_tensor(g.e[:, :], g.e[:, :], g.adj[:, :], ALU.add))
                    else:
                        step(dve.tensor_tensor(g.e[:, :], g.e[:, :], g.adj[:, :], ALU.mult))
                    step(dve.reduce_max(g.top[:, 0:1], g.e[:, :], AX_X))
                    dve.tensor_scalar(g.top[:, 1:2], g.top[:, 0:1], -1.0, None, ALU.mult).then_inc(shifted, 1)
                    for c in range(NCH):
                        dve.wait_ge(turned, k * NCH + c + 1)
                        if c >= 2:
                            dve.wait_ge(summed, k * NCH + c - 1)
                        dve.tensor_copy(g.p_t[:, c % 2, :], m.psum[c % 2][:, :]).then_inc(turn_copied, 1)
                    dve.wait_ge(summed, k * NCH + NCH)
                    dve.reciprocal(g.top[:, 3:4], g.top[:, 2:3]).then_inc(normed, 1)
                    dve.wait_ge(normed, 2 * k + 1)
                    dve.tensor_scalar(g.att[:, bass.ds(i, 1), bass.ds(h * dh, dh)], m.psum[3][:, 0:dh],
                                      g.top[:, 3:4], None, ALU.mult).then_inc(normed, 1)
                    dve.wait_ge(normed, 2 * k + 2)

        @block.scalar
        def _(act):
            with act.Fori(0, heads) as h:
                for c in range(NCH):
                    act.wait_ge(spread_done, h * NCH + c + 1)
                    act.activation(g.row[:, c * CHUNK:(c + 1) * CHUNK], m.psum[2][:, :], ACT.Copy).then_inc(row_done, 1)
                with act.Fori(0, T) as i:
                    k = h * T + i
                    act.wait_ge(shifted, k + 1)
                    act.activation(g.e[:, :], g.e[:, :], ACT.Exp, bias=g.top[:, 1:2],
                                   accum_out=g.top[:, 2:3]).then_inc(exp_done, 1)

        @block.tensor
        def _(pe):
            with pe.Fori(0, heads) as h:
                for c in range(NCH):
                    pe.wait_ge(diag_done, h * NCH + c + 1)
                    if c:
                        pe.wait_ge(row_done, h * NCH + c)
                    pe.matmul(m.psum[2][:, :], m.ones[:, :], g.diag[:, :, :], start=True, stop=True).then_inc(spread_done, 1)
                with pe.Fori(0, T) as i:
                    k = h * T + i

                    def turn(c):
                        if c >= 2:
                            pe.wait_ge(turn_copied, k * NCH + c - 1)
                        for b in range(BPC):
                            last = pe.transpose(m.psum[c % 2][:, b * P:(b + 1) * P],
                                                g.e[:, c * CHUNK + b * P:c * CHUNK + (b + 1) * P], m.ident[:, :])
                        last.then_inc(turned, 1)
                    pe.wait_ge(exp_done, k + 1)
                    turn(0)
                    for c in range(NCH):
                        if c + 1 < NCH:
                            turn(c + 1)
                        pe.wait_ge(turn_copied, k * NCH + c + 1)
                        for b in range(BPC):
                            blk = c * BPC + b
                            last = pe.matmul(m.psum[3][:, 0:dh], g.p_t[:, c % 2, b * P:(b + 1) * P],
                                             m.table[:, blk, bass.ds(h * dh, dh)], start=blk == 0, stop=blk == T - 1)
                        last.then_inc(summed, 1)


def finish_any(nc, ctx, m, layer, out, g, tag):
    def sem(name):
        return ctx.enter_context(nc.semaphore(name + tag))

    low, exp_done, high, added, written = sem("low"), sem("exp_done"), sem("high"), sem("added"), sem("written")
    flat = g.att[:, :, :].rearrange("p t d -> p (t d)")
    x_flat = m.x_sb[:, :, :].rearrange("p t d -> p (t d)")
    with nc.Block() as block:
        @block.vector
        def _(dve):
            if layer == 0:
                dve.tensor_scalar(g.e[:, :], flat, 0.0, None, ALU.min).then_inc(low, 1)
                dve.tensor_scalar(flat, flat, 0.0, -1.0, ALU.max, ALU.add).then_inc(high, 1)
                dve.wait_ge(high, 1)
                dve.wait_ge(exp_done, 1)
                dve.tensor_tensor(flat, flat, g.e[:, :], ALU.add).then_inc(high, 1)
                dve.wait_ge(high, 2)
            dve.tensor_tensor(x_flat, x_flat, flat, ALU.add).then_inc(added, 1)

        @block.scalar
        def _(act):
            if layer == 0:
                act.wait_ge(low, 1)
                act.activation(g.e[:, :], g.e[:, :], ACT.Exp).then_inc(exp_done, 1)

        @block.sync
        def _(sp):
            if layer == 1:
                sp.wait_ge(added, 1)
                sp.dma_start(out.rearrange("(t p) d -> p t d", p=P), m.x_sb[:, :, :]).then_inc(written, 16)
                sp.wait_ge(written, 16)


def allocate_sparse(nc, ctx):
    f = Memory()

    def sb(name, shape, dt=F32):
        return ctx.enter_context(nc.sbuf_tensor(name, shape, dt))

    f.adj = sb("adj_rows", [P, 3, N])
    f.sign = sb("sign", [P, 2, N], BF16)
    f.hit = sb("hit", [P, P], BF16)
    f.ones_b = sb("ones_b", [64, P], BF16)
    f.column = sb("column", [64, N], BF16)
    f.before = sb("before", [P, P])
    f.edge_no = sb("edge_no", [P, E])
    f.my_edge = sb("my_edge", [P, EC, K])
    f.slot_no = sb("slot_no", [P, K])
    f.self_key = sb("self_key", [P, T])
    f.ints = sb("ints", [P, E], I32)
    f.sign_sum = sb("sign_sum", [P, T, 2])
    f.cand = sb("cand", [P, 2, CAND])
    f.last_found = sb("last_found", [P, T, NSEG])
    f.rest = sb("rest", [P, CAND])
    f.scrap = sb("scrap", [P, CAND])
    f.scrap2 = sb("scrap2", [P, K])
    f.degree = sb("degree", [P, T])
    f.first = sb("first", [P, T])
    f.end = sb("end", [P, T])
    f.has_self = sb("has_self", [P, T])
    f.rows = sb("rows", [P, 2 * K])
    f.rows_b = sb("rows_b", [P, 2, 2 * K], BF16)
    f.score_b = sb("score_b", [P, 3, T, 2 * H1], BF16)
    f.score_r = sb("score_r", [P, 1, T * 2 * H1])
    f.ident_b = sb("ident_b", [P, P], BF16)
    f.row_scores = sb("row_scores", [P, T, 2 * H0])
    f.self_sum = sb("self_sum", [P, T, 2 * H0])
    f.ahead = sb("ahead", [P, 2, E])
    f.member = sb("member", [P, 2, E], BF16)
    f.member_t = sb("member_t", [P, 2, EC, P])
    f.is_slot = sb("is_slot", [P, EC, K])
    f.slot_val = sb("slot_val", [P, EC, K])
    f.key = sb("key", [P, EC])
    f.index = sb("index", [P, T, EC], U32)
    f.edge_row = sb("edge_row", [P, 2, EC, 2 * H1])
    f.gathered = sb("gathered", [P, 2, EC, G1])
    f.pair = sb("pair", [P, EC, 2 * H1])
    f.logit = sb("logit", [P, EC, H1])
    f.value = sb("value", [P, 2, EC, V1])
    f.sums = sb("sums", [P, T * V1])
    f.den = sb("den", [P, T, H1])
    f.total = sb("total", [P, D])
    f.self_w = sb("self_w", [P, T])
    f.full = sb("full", [P, 8])
    f.full_sum = sb("full_sum", [P, 1])
    f.flag = sb("flag", [1, 1], I32)
    f.t0 = nc.dram_tensor("node_table0", (N, G0), F32).ap()
    f.t1 = nc.dram_tensor("node_table1", (N, G1), F32).ap()
    return f


def one(i):
    return bass.ds(i, 1)


def sparse_constants(nc, ctx, m, f):
    def sem(name):
        return ctx.enter_context(nc.semaphore(name))

    filled, copied = sem("filled"), sem("copied")
    wide = f.adj[:, 0, :].bitcast(I32)
    with nc.Block() as block:
        @block.gpsimd
        def _(pool):
            pool.memset(f.hit[:, :], 0.0).then_inc(filled, 1)
            pool.memset(f.ones_b[:, :], 1.0).then_inc(filled, 1)
            pool.memset(f.before[:, :], 1.0).then_inc(filled, 1)
            pool.iota(f.ints[:, :], [[1, E]], base=0, channel_multiplier=0).then_inc(filled, 1)
            pool.iota(wide[0:1, :], [[64, N // 64], [0, 64]], base=0, channel_multiplier=0).then_inc(filled, 1)
            pool.wait_ge(filled, 5)
            pool.iota(wide[32:33, :], [[0, N // 64], [1, 64]], base=0, channel_multiplier=0).then_inc(filled, 1)
            pool.wait_ge(filled, 6)
            pool.iota(f.adj[:, 1, 0:EC * K].bitcast(I32), [[P, EC], [0, K]], base=0, channel_multiplier=1).then_inc(filled, 1)
            pool.iota(f.adj[:, 2, 0:T].bitcast(I32), [[P, T]], base=N, channel_multiplier=1).then_inc(filled, 1)
            pool.wait_ge(filled, 8)
            pool.affine_select(out=f.hit[:, :], in_=f.hit[:, :], compare_op=ALU.not_equal, fill=HIT,
                               base=0, pattern=[[-1, P]], channel_multiplier=1).then_inc(filled, 1)
            pool.affine_select(out=f.before[:, :], in_=f.before[:, :], compare_op=ALU.is_gt, fill=0.0,
                               base=0, pattern=[[1, P]], channel_multiplier=-1).then_inc(filled, 1)

        @block.vector
        def _(dve):
            dve.memset(f.column[:, :], 0.0).then_inc(copied, 1)
            dve.wait_ge(filled, 10)
            dve.wait_ge(copied, 1)
            dve.tensor_copy(f.column[0:1, :], wide[0:1, :]).then_inc(copied, 1)
            dve.tensor_copy(f.column[32:33, :], wide[32:33, :]).then_inc(copied, 1)
            dve.tensor_copy(f.edge_no[:, :], f.ints[:, :]).then_inc(copied, 1)
            dve.tensor_copy(f.slot_no[:, :], f.ints[:, 0:K]).then_inc(copied, 1)
            dve.tensor_copy(f.my_edge[:, :, :], f.adj[:, 1, 0:EC * K].bitcast(I32).rearrange("p (c k) -> p c k", c=EC)).then_inc(copied, 1)
            dve.tensor_copy(f.self_key[:, :], f.adj[:, 2, 0:T].bitcast(I32)).then_inc(copied, 1)
            dve.tensor_copy(f.ident_b[:, :], m.ident[:, :]).then_inc(copied, 1)
            dve.wait_ge(copied, 8)


def publish(nc, ctx, m, f, layer):
    def sem(name):
        return ctx.enter_context(nc.semaphore(f"{name}_publish{layer}"))

    sent, made, summed, folded = sem("sent"), sem("made"), sem("summed"), sem("folded")
    dest, cols = (f.t0, G0) if layer == 0 else (f.t1, G1)
    split_done = sem("split_done")

    def split(dve, scores, width):
        part = [f.score_b[:, k, :, 0:width] for k in range(3)]
        left = [f.score_r[:, k, 0:T * width].rearrange("p (t w) -> p t w", t=T) for k in range(1)]
        dve.tensor_copy(part[0], scores).then_inc(split_done, 1)
        dve.wait_ge(split_done, 1)
        dve.tensor_tensor(left[0], scores, part[0], ALU.subtract).then_inc(split_done, 1)
        dve.wait_ge(split_done, 2)
        dve.tensor_copy(part[1], left[0]).then_inc(split_done, 1)
        dve.wait_ge(split_done, 3)
        dve.tensor_tensor(part[2], left[0], part[1], ALU.subtract).then_inc(split_done, 1)
        dve.wait_ge(split_done, 4)

    with nc.Block() as block:
        @block.sync
        def _(sp):
            sp.dma_start(dest.rearrange("(t p) c -> p t c", p=P), m.table[:, :, 0:cols]).then_inc(sent, 16)
            sp.wait_ge(sent, 16)

        if layer == 0:
            @block.vector
            def _(dve):
                dve.tensor_tensor(f.self_sum[:, :, :], m.table[:, :, D:D + 2 * H0], m.table[:, :, D + 2 * H0:S0],
                                  ALU.add).then_inc(made, 1)
                dve.wait_ge(made, 1)
                dve.tensor_tensor(f.self_sum[:, :, 0:H0], f.self_sum[:, :, 0:H0], f.self_sum[:, :, H0:2 * H0],
                                  ALU.max).then_inc(made, 1)
                dve.wait_ge(made, 2)
                for half in range(2):
                    dve.tensor_tensor(f.row_scores[:, :, half * H0:(half + 1) * H0],
                                      m.table[:, :, D + (2 + half) * H0:D + (3 + half) * H0],
                                      f.self_sum[:, :, 0:H0], ALU.subtract).then_inc(made, 1)
                dve.wait_ge(made, 4)
                split(dve, f.row_scores[:, :, :], 2 * H0)
        else:
            @block.tensor
            def _(pe):
                for c in range(NCH):
                    last = pe.matmul(m.psum[0][:, :], m.ones[:, :], m.table[:, c * BPC:(c + 1) * BPC, 0:D],
                                     start=c == 0, stop=c == NCH - 1)
                last.then_inc(summed, 1)

            @block.vector
            def _(dve):
                split(dve, m.table[:, :, D + 2 * H1:S1], 2 * H1)
                dve.wait_ge(summed, 1)
                dve.reduce_sum(f.total[:, :], m.psum[0][:, :].rearrange("p (b d) -> p d b", b=BPC), AX_X).then_inc(folded, 1)
                dve.wait_ge(folded, 1)


def find_and_attend0(nc, ctx, m, f, adj):
    def sem(name):
        return ctx.enter_context(nc.semaphore(name))

    a_loaded = [sem("a_loaded0"), sem("a_loaded1")]
    signed, keyed, searched = sem("signed"), sem("keyed"), sem("searched")
    counted, ranked, placed, bounded, ahead_done = (
        sem("counted"), sem("ranked"), sem("placed"), sem("bounded"), sem("ahead_done"))
    member_done, spread, turned, member_t_done = sem("member_done"), sem("spread"), sem("turned_edges"), sem("member_t_done")
    picking, indexed, row_copied = sem("picking"), sem("indexed"), sem("row_copied")
    gathered = [sem("gathered0"), sem("gathered1")]
    paired, logits_done, weighed, valued, summed, stored = (
        sem("paired"), sem("logits_done"), sem("weighed"), sem("valued"), sem("summed"), sem("sums_stored"))

    kept, passed, shown, parted = sem("kept"), sem("passed"), sem("shown"), sem("parted")
    key_bank = [m.psum_all[:, 0:SEG], m.psum_all[:, SEG:2 * SEG]]
    place_ps = m.psum[4][:, 0:1]
    spread_ps = m.psum[5][:, 0:EC * 40].rearrange("p (c k) -> p c k", c=EC)
    turn_ps = m.psum[6][:, 0:EC * P // 2].bitcast(BF16)
    sum_ps = m.psum[7][:, 0:V0]
    W = 2 * K + 2 * H0
    ACC = EC * 16

    def steps(engine, step):
        for i in range(4):
            step(i, i % 2, i // 2, i < T, i >= 1, i >= 3)
        with engine.Fori(2, T // 2 - 1) as j:
            for u in range(2):
                step(2 * j + u, u, j, True, True, True)
        for i in range(T - 2, T + 3):
            step(i, i % 2, i // 2, i < T, i - 1 < T, True)

    def past(i, n):
        return not isinstance(i, int) or i >= n

    with nc.Block() as block:
        @block.sync
        def _(sp):
            def load(i, u):
                sp.dma_start(f.adj[:, u, :], adj[bass.ds(i * P, P), :]).then_inc(a_loaded[u], 16)
            load(0, 0)
            load(1, 1)
            with sp.Fori(1, T // 2) as j:
                for u in range(2):
                    sp.wait_ge(signed, 2 * (2 * j + u - 1))
                    load(2 * j + u, u)

        @block.scalar
        def _(act):
            def sign(i, u, j, half):
                if half == 0:
                    act.wait_ge(a_loaded[u], 16 * j + 16)
                    if past(i, 2):
                        act.wait_ge(keyed, NSEG * (i - 1))
                cols = slice(half * N // 2, (half + 1) * N // 2)
                act.activation(f.sign[:, u, cols], f.adj[:, u, cols], ACT.Sign,
                               accum_out=f.sign_sum[:, one(i), half:half + 1]).then_inc(signed, 1)

            def step(i, u, j, search, pack, attend):
                more = not isinstance(i, int) or i + 1 < T
                v = 1 - u
                if attend:
                    act.wait_ge(logits_done, i - 2)
                    if past(i, 5):
                        act.wait_ge(summed, i - 4)
                    act.activation(f.value[:, v, :, D:V0], f.logit[:, :, 0:H0], ACT.Exp).then_inc(weighed, 1)
                if pack:
                    act.wait_ge(bounded, 2 * i)
                    if past(i, 3):
                        act.wait_ge(member_done, i - 2)
                    act.activation(f.ahead[:, v, :], f.edge_no[:, :], ACT.Relu, scale=-1.0,
                                   bias=f.first[:, one(i - 1)]).then_inc(ahead_done, 1)
                if more:
                    sign(i + 1, v, j + u, 0)
                if more:
                    sign(i + 1, v, j + u, 1)
                if attend:
                    act.wait_ge(summed, i - 2)
                    act.activation(f.sums[:, bass.ds((i - 3) * V0, V0)], sum_ps, ACT.Copy).then_inc(stored, 1)
                if pack:
                    act.wait_ge(turned, i)
                    if past(i, 3):
                        act.wait_ge(summed, i - 2)
                    act.activation(f.member_t[:, v, :, :], turn_ps, ACT.Copy).then_inc(member_t_done, 1)
            sign(0, 0, 0, 0)
            sign(0, 0, 0, 1)
            steps(act, step)

        @block.tensor
        def _(pe):
            def keys(i, u, seg):
                pe.wait_ge(signed, 2 * i + 1 + seg // 2)
                if past(i, 1) or seg >= 2:
                    pe.wait_ge(searched, NSEG * i + seg - 1)
                for b in range(2):
                    cols = slice(seg * SEG + b * CHUNK, seg * SEG + (b + 1) * CHUNK)
                    out_ps = key_bank[seg % 2][:, b * CHUNK:(b + 1) * CHUNK]
                    pe.matmul(out_ps, f.hit[:, :], f.sign[:, u, cols], start=True, stop=False)
                    last = pe.matmul(out_ps, f.ones_b[:, :], f.column[:, cols], start=False, stop=True)
                last.then_inc(keyed, 1)

            def step(i, u, j, search, pack, attend):
                v = 1 - u
                if search:
                    keys(i, u, 0)
                    keys(i, u, 1)
                if pack:
                    pe.wait_ge(counted, i)
                    if past(i, 2):
                        pe.wait_ge(bounded, 2 * (i - 1))
                    pe.matmul(place_ps, f.before[:, :], f.degree[:, one(i - 1)], start=True, stop=True).then_inc(placed, 1)
                if search:
                    keys(i, u, 2)
                    keys(i, u, 3)
                if pack:
                    pe.wait_ge(member_done, i)
                    pe.wait_ge(parted, 2 * i)
                    if past(i, 2):
                        pe.wait_ge(row_copied, i - 1)
                        pe.wait_ge(member_t_done, i - 1)
                    for c in range(EC):
                        edges = f.member[:, v, c * P:(c + 1) * P]
                        for k in range(2):
                            pe.matmul(spread_ps[:, c, 0:2 * K], edges, f.rows_b[:, k, :], start=k == 0, stop=k == 1)
                        for k in range(3):
                            last = pe.matmul(spread_ps[:, c, 2 * K:W], edges, f.score_b[:, k, one(i - 1), 0:2 * H0],
                                             start=k == 0, stop=k == 2)
                    last.then_inc(spread, 1)
                    for c in range(EC):
                        last = pe.transpose(turn_ps[:, c * P:(c + 1) * P], f.member[:, v, c * P:(c + 1) * P],
                                            f.ident_b[:, :])
                    last.then_inc(turned, 1)
                if attend:
                    pe.wait_ge(valued, i - 2)
                    pe.wait_ge(weighed, i - 2)
                    pe.wait_ge(member_t_done, i - 2)
                    if past(i, 4):
                        pe.wait_ge(stored, i - 3)
                    for c in range(EC):
                        last = pe.matmul(sum_ps, f.member_t[:, v, c, :], f.value[:, v, c, 0:V0],
                                         start=c == 0, stop=c == EC - 1)
                    last.then_inc(summed, 1)
            steps(pe, step)

        @block.vector
        def _(dve):
            def wait_apart(semaphore, value):
                dve.wait_ge(semaphore, value)
                if not isinstance(value, int):
                    dve.sem_inc(passed, 1)

            def search(i, u, seg):
                if past(i, 2) and seg == 0:
                    wait_apart(kept, i - 1)
                wait_apart(keyed, NSEG * i + seg + 1)
                dve.max(f.cand[:, u, seg * FOUND:(seg + 1) * FOUND], key_bank[seg % 2]).then_inc(searched, 1)

            def pick_and_rank(i, u, do_pick, do_rank):
                row = f.cand[:, u, :]
                if do_rank:
                    dve.wait_ge(searched, NSEG * (i + 1))
                    if past(i, 1):
                        dve.wait_ge(spread, i)
                    dve.tensor_scalar(f.scrap[:, :], row, HIT, 0.0, ALU.is_ge, ALU.add,
                                      accum_out=f.degree[:, one(i)]).then_inc(counted, 1)
                if do_pick:
                    dve.wait_ge(spread, i)
                    dve.tensor_tensor(f.is_slot[:, :, :], f.my_edge[:, :, :], spread_ps[:, :, K:2 * K],
                                      ALU.is_equal).then_inc(picking, 1)
                if do_rank:
                    dve.max(f.rows[:, 0:FOUND], row).then_inc(ranked, 1)
                if do_pick:
                    dve.wait_ge(picking, 3 * (i - 1) + 1)
                    dve.tensor_tensor(f.slot_val[:, :, :], f.is_slot[:, :, :], spread_ps[:, :, 0:K],
                                      ALU.mult).then_inc(picking, 1)
                if do_rank:
                    wait_apart(ranked, 4 * i + 1)
                    dve.match_replace(f.rest[:, :], f.rows[:, 0:FOUND], row, 0.0).then_inc(ranked, 1)
                if do_pick:
                    dve.wait_ge(picking, 3 * (i - 1) + 2)
                    dve.reduce_sum(f.key[:, :], f.slot_val[:, :, :], AX_X).then_inc(picking, 1)
                if do_rank:
                    wait_apart(ranked, 4 * i + 2)
                    dve.max(f.rows[:, FOUND:K], f.rest[:, :]).then_inc(ranked, 1)
                if do_pick:
                    dve.wait_ge(picking, 3 * (i - 1) + 3)
                    dve.tensor_scalar(f.index[:, one(i - 1), :], f.key[:, :], -HIT, 0.0, ALU.add, ALU.max).then_inc(indexed, 1)
                if do_rank:
                    dve.tensor_copy(f.last_found[:, one(i), :], row.rearrange("p (s k) -> p s k", k=FOUND)[:, :, FOUND - 1]
                                    ).then_inc(kept, 1)
                    dve.wait_ge(ranked, 4 * i + 3)
                    dve.tensor_scalar(f.scrap2[:, :], f.rows[:, 0:K], f.self_key[:, one(i)], 0.0, ALU.is_equal, ALU.add,
                                      accum_out=f.has_self[:, one(i)]).then_inc(ranked, 1)
                if do_pick:
                    dve.tensor_copy(f.edge_row[:, 1 - u, :, 0:2 * H0], spread_ps[:, :, 2 * K:W]).then_inc(row_copied, 1)

            def step(i, u, j, do_search, pack, attend):
                v = 1 - u
                if attend:
                    dve.wait_ge(gathered[v], ACC * (j + u - 1))
                    dve.wait_ge(row_copied, i - 2)
                    if past(i, 4):
                        dve.wait_ge(weighed, i - 3)
                        dve.wait_ge(logits_done, i - 3)
                    dve.tensor_tensor(f.pair[:, :, 0:2 * H0], f.gathered[:, v, :, D:G0], f.edge_row[:, v, :, 0:2 * H0],
                                      ALU.add).then_inc(paired, 1)
                    dve.wait_ge(paired, i - 2)
                    dve.tensor_tensor(f.logit[:, :, 0:H0], f.pair[:, :, 0:H0], f.pair[:, :, H0:2 * H0],
                                      ALU.max).then_inc(logits_done, 1)
                if do_search:
                    search(i, u, 0)
                if pack:
                    dve.wait_ge(placed, i)
                    dve.wait_ge(counted, i)
                    dve.tensor_copy(f.first[:, one(i - 1)], place_ps).then_inc(bounded, 1)
                    dve.tensor_tensor(f.end[:, one(i - 1)], place_ps, f.degree[:, one(i - 1)], ALU.add).then_inc(bounded, 1)
                    dve.wait_ge(bounded, 2 * i)
                    dve.tensor_scalar(f.rows[:, K:2 * K], f.slot_no[:, :], f.first[:, one(i - 1)], None,
                                      ALU.add).then_inc(shown, 1)
                if do_search:
                    search(i, u, 1)
                if pack:
                    dve.wait_ge(shown, i)
                    dve.wait_ge(ranked, 4 * i)
                    dve.tensor_copy(f.rows_b[:, 0, :], f.rows[:, :]).then_inc(parted, 1)
                if pack:
                    dve.wait_ge(ahead_done, i)
                    if past(i, 3):
                        dve.wait_ge(turned, i - 2)
                    dve.scalar_tensor_tensor(out=f.member[:, v, :], in0=f.edge_no[:, :], scalar=f.end[:, one(i - 1)],
                                             in1=f.ahead[:, v, :], op0=ALU.is_lt, op1=ALU.is_gt).then_inc(member_done, 1)
                if pack:
                    dve.wait_ge(parted, 2 * i - 1)
                    dve.tensor_tensor(f.rows_b[:, 1, :], f.rows[:, :], f.rows_b[:, 0, :], ALU.subtract).then_inc(parted, 1)
                if do_search:
                    search(i, u, 2)
                if do_search:
                    search(i, u, 3)
                pick_and_rank(i, u, pack, do_search)
            steps(dve, step)

        @block.gpsimd
        def _(pool):
            def weigh(t, v):
                pool.wait_ge(weighed, t + 1)
                if t >= 2:
                    pool.wait_ge(summed, t - 1)
                pool.tensor_tensor(
                    f.value[:, v, :, 0:D].rearrange("p c (h d) -> p c h d", h=H0),
                    f.gathered[:, v, :, 0:D].rearrange("p c (h d) -> p c h d", h=H0),
                    f.value[:, v, :, D:V0][:, :, :, None].to_broadcast([P, EC, H0, D0]),
                    ALU.mult).then_inc(valued, 1)

            def gather(t, v):
                pool.wait_ge(indexed, t + 1)
                if past(t, 2):
                    pool.wait_ge(valued, t - 1)
                for c in range(EC):
                    pool.indirect_dma_start(out=f.gathered[:, v, c, 0:G0], out_offset=None, in_=f.t0[:, :],
                                            in_offset=bass.IndirectOffsetOnAxis(ap=f.index[:, t, c:c + 1], axis=0)
                                            ).then_inc(gathered[v], 16)
            for t in range(T + 2):
                if t >= 2:
                    weigh(t - 2, t % 2)
                if t < T:
                    gather(t, t % 2)


def finish0(nc, ctx, m, f):
    def sem(name):
        return ctx.enter_context(nc.semaphore(name))

    chain, low, exp_done = sem("finish0_chain"), sem("finish0_low"), sem("finish0_exp")
    sums = f.sums[:, 0:T * V0].rearrange("p (t v) -> p t v", t=T)
    part = f.adj[:, 0, :].rearrange("p (t d) -> p t d", t=T)
    neg = f.adj[:, 1, :].rearrange("p (t d) -> p t d", t=T)
    with nc.Block() as block:
        @block.vector
        def _(dve):
            at = [0]

            def link(ins):
                at[0] += 1
                ins.then_inc(chain, 1)
                dve.wait_ge(chain, at[0])
            link(dve.tensor_scalar(f.self_w[:, :], f.has_self[:, :], -1.0, 1.0, ALU.mult, ALU.add))
            link(dve.tensor_tensor(part, m.table[:, :, 0:D], f.self_w[:, :, None].to_broadcast([P, T, D]), ALU.mult))
            link(dve.tensor_tensor(part, part, sums[:, :, 0:D], ALU.add))
            link(dve.tensor_tensor(f.den[:, :, 0:H0], sums[:, :, D:V0], f.self_w[:, :, None].to_broadcast([P, T, H0]), ALU.add))
            link(dve.tensor_scalar(f.sums[:, 0:T * H0].rearrange("p (t h) -> p t h", t=T), f.den[:, :, 0:H0], DEN_MAX, 0.0,
                                   ALU.is_le, ALU.add, accum_out=f.full[:, 0:1]))
            link(dve.reciprocal(f.den[:, :, 0:H0], f.den[:, :, 0:H0]))
            for h in range(H0):
                dve.tensor_tensor(part[:, :, h * D0:(h + 1) * D0], part[:, :, h * D0:(h + 1) * D0],
                                  f.den[:, :, h:h + 1].to_broadcast([P, T, D0]), ALU.mult).then_inc(chain, 1)
            at[0] += H0
            dve.wait_ge(chain, at[0])
            dve.tensor_scalar(neg, part, 0.0, None, ALU.min).then_inc(low, 1)
            link(dve.tensor_scalar(part, part, 0.0, -1.0, ALU.max, ALU.add))
            link(dve.tensor_tensor(m.x_sb[:, :, :], m.x_sb[:, :, :], part, ALU.add))
            dve.wait_ge(exp_done, 1)
            link(dve.tensor_tensor(m.x_sb[:, :, :], m.x_sb[:, :, :], neg, ALU.add))

        @block.scalar
        def _(act):
            act.wait_ge(low, 1)
            act.activation(neg, neg, ACT.Exp).then_inc(exp_done, 1)


def attend1(nc, ctx, m, f):
    def sem(name):
        return ctx.enter_context(nc.semaphore(name + "_l1"))

    ahead_done, member_done, spread, turned, member_t_done, row_copied = (
        sem("ahead_done"), sem("member_done"), sem("spread"), sem("turned"), sem("member_t_done"), sem("row_copied"))
    gathered = [sem("gathered0"), sem("gathered1")]
    paired, logits_done, weighed, less_one, valued, summed, stored = (
        sem("paired"), sem("logits_done"), sem("weighed"), sem("less_one"), sem("valued"), sem("summed"), sem("stored"))
    spread_ps = m.psum[5][:, 0:EC * 2 * H1].rearrange("p (c k) -> p c k", c=EC)
    turn_ps = m.psum[6][:, 0:EC * P // 2].bitcast(BF16)
    sum_ps = m.psum[7][:, 0:V1]
    ACC = EC * 16

    def steps(engine, step):
        for i in range(4):
            step(i, i % 2, i // 2, True, i >= 1)
        with engine.Fori(2, T // 2 - 1) as j:
            for u in range(2):
                step(2 * j + u, u, j, True, True)
        for i in range(T - 2, T + 1):
            step(i, i % 2, i // 2, i < T, True)

    def past(i, n):
        return not isinstance(i, int) or i >= n

    with nc.Block() as block:
        @block.scalar
        def _(act):
            def lead(i, u):
                if past(i, 2):
                    act.wait_ge(member_done, i - 1)
                act.activation(f.ahead[:, u, :], f.edge_no[:, :], ACT.Relu, scale=-1.0,
                               bias=f.first[:, one(i)]).then_inc(ahead_done, 1)

            def step(i, u, j, pack, attend):
                v = 1 - u
                if attend:
                    act.wait_ge(logits_done, i)
                    if past(i, 2):
                        act.wait_ge(less_one, i - 1)
                    act.activation(f.pair[:, :, 0:H1], f.logit[:, :, :], ACT.Exp).then_inc(weighed, 1)
                if pack and (not isinstance(i, int) or i + 1 < T):
                    lead(i + 1, v)
                if pack:
                    act.wait_ge(turned, i + 1)
                    if past(i, 2):
                        act.wait_ge(summed, i - 1)
                    act.activation(f.member_t[:, u, :, :], turn_ps, ACT.Copy).then_inc(member_t_done, 1)
                if attend:
                    act.wait_ge(summed, i)
                    act.activation(f.sums[:, bass.ds((i - 1) * V1, V1)], sum_ps, ACT.Copy).then_inc(stored, 1)
            lead(0, 0)
            steps(act, step)

        @block.tensor
        def _(pe):
            def step(i, u, j, pack, attend):
                v = 1 - u
                if pack:
                    pe.wait_ge(member_done, i + 1)
                    if past(i, 1):
                        pe.wait_ge(row_copied, i)
                        pe.wait_ge(member_t_done, i)
                    for c in range(EC):
                        for k in range(3):
                            last = pe.matmul(spread_ps[:, c, :], f.member[:, u, c * P:(c + 1) * P],
                                             f.score_b[:, k, one(i), :], start=k == 0, stop=k == 2)
                    last.then_inc(spread, 1)
                    for c in range(EC):
                        last = pe.transpose(turn_ps[:, c * P:(c + 1) * P], f.member[:, u, c * P:(c + 1) * P],
                                            f.ident_b[:, :])
                    last.then_inc(turned, 1)
                if attend:
                    pe.wait_ge(valued, i)
                    pe.wait_ge(member_t_done, i)
                    if past(i, 2):
                        pe.wait_ge(stored, i - 1)
                    for c in range(EC):
                        last = pe.matmul(sum_ps, f.member_t[:, v, c, :], f.value[:, v, c, :], start=c == 0, stop=c == EC - 1)
                    last.then_inc(summed, 1)
            steps(pe, step)

        @block.vector
        def _(dve):
            def step(i, u, j, pack, attend):
                v = 1 - u
                if attend:
                    dve.wait_ge(gathered[v], ACC * (j + u))
                    dve.wait_ge(row_copied, i)
                    if past(i, 2):
                        dve.wait_ge(less_one, i - 1)
                    dve.tensor_tensor(f.value[:, v, :, 0:2 * H1], f.gathered[:, v, :, D:G1], f.edge_row[:, v, :, :],
                                      ALU.add).then_inc(paired, 1)
                    dve.wait_ge(paired, i)
                    dve.tensor_tensor(f.logit[:, :, :], f.value[:, v, :, 0:H1], f.value[:, v, :, H1:2 * H1],
                                      ALU.max).then_inc(logits_done, 1)
                if pack:
                    dve.wait_ge(ahead_done, i + 1)
                    if past(i, 2):
                        dve.wait_ge(turned, i - 1)
                    dve.scalar_tensor_tensor(out=f.member[:, u, :], in0=f.edge_no[:, :], scalar=f.end[:, one(i)],
                                             in1=f.ahead[:, u, :], op0=ALU.is_lt, op1=ALU.is_gt).then_inc(member_done, 1)
                if attend:
                    dve.wait_ge(weighed, i)
                    dve.wait_ge(logits_done, i)
                    if past(i, 3):
                        dve.wait_ge(summed, i - 2)
                    dve.tensor_scalar(f.value[:, v, :, D:V1], f.pair[:, :, 0:H1], 1.0, None, ALU.subtract).then_inc(less_one, 1)
                    dve.wait_ge(less_one, i)
                    dve.tensor_tensor(
                        f.value[:, v, :, 0:D].rearrange("p c (h d) -> p c h d", h=H1),
                        f.gathered[:, v, :, 0:D].rearrange("p c (h d) -> p c h d", h=H1),
                        f.value[:, v, :, D:V1][:, :, :, None].to_broadcast([P, EC, H1, D1]),
                        ALU.mult).then_inc(valued, 1)
                if pack:
                    dve.wait_ge(spread, i + 1)
                    dve.tensor_copy(f.edge_row[:, u, :, :], spread_ps).then_inc(row_copied, 1)
            steps(dve, step)

        @block.gpsimd
        def _(pool):
            for t in range(T):
                if t >= 2:
                    pool.wait_ge(valued, t - 1)
                for c in range(EC):
                    pool.indirect_dma_start(out=f.gathered[:, t % 2, c, 0:G1], out_offset=None, in_=f.t1[:, :],
                                            in_offset=bass.IndirectOffsetOnAxis(ap=f.index[:, t, c:c + 1], axis=0)
                                            ).then_inc(gathered[t % 2], 16)


def finish1(nc, ctx, m, f, out):
    def sem(name):
        return ctx.enter_context(nc.semaphore(name))

    chain, added, written, tallied, flagged = (
        sem("finish1_chain"), sem("finish1_added"), sem("written"), sem("tallied"), sem("flagged"))
    sums = f.sums[:, 0:T * V1].rearrange("p (t v) -> p t v", t=T)
    part = f.adj[:, 0, :].rearrange("p (t d) -> p t d", t=T)
    scrap = f.adj[:, 1, :]
    with nc.Block() as block:
        @block.vector
        def _(dve):
            at = [0]

            def link(ins):
                at[0] += 1
                ins.then_inc(chain, 1)
                dve.wait_ge(chain, at[0])
            link(dve.tensor_scalar(f.den[:, :, :], sums[:, :, D:V1], float(N), None, ALU.add))
            link(dve.tensor_scalar(scrap[:, 0:T * H1].rearrange("p (t h) -> p t h", t=T), f.den[:, :, :], DEN_MAX, 0.0,
                                   ALU.is_le, ALU.add, accum_out=f.full[:, 1:2]))
            link(dve.reciprocal(f.den[:, :, :], f.den[:, :, :]))
            link(dve.tensor_tensor(part, sums[:, :, 0:D], f.total[:, None, :].to_broadcast([P, T, D]), ALU.add))
            for h in range(H1):
                dve.tensor_tensor(part[:, :, h * D1:(h + 1) * D1], part[:, :, h * D1:(h + 1) * D1],
                                  f.den[:, :, h:h + 1].to_broadcast([P, T, D1]), ALU.mult).then_inc(chain, 1)
            at[0] += H1
            dve.wait_ge(chain, at[0])
            dve.tensor_tensor(m.x_sb[:, :, :], m.x_sb[:, :, :], part, ALU.add).then_inc(added, 1)
            link(dve.tensor_scalar(scrap[:, 0:T * NSEG], f.last_found[:, :, :].rearrange("p t s -> p (t s)"), HIT, 0.0, ALU.is_lt, ALU.add, accum_out=f.full[:, 2:3]))
            link(dve.tensor_scalar(scrap[:, 0:T], f.degree[:, :], float(K), 0.0, ALU.is_le, ALU.add, accum_out=f.full[:, 3:4]))
            link(dve.tensor_scalar(scrap[:, 0:T], f.end[:, :], float(E), 0.0, ALU.is_le, ALU.add, accum_out=f.full[:, 4:5]))
            link(dve.tensor_tensor(scrap[:, 0:T], f.sign_sum[:, :, 0], f.sign_sum[:, :, 1], ALU.add))
            link(dve.tensor_tensor(scrap[:, 0:T], scrap[:, 0:T], f.degree[:, :], ALU.is_equal))
            link(dve.reduce_sum(f.full[:, 5:6], scrap[:, 0:T], AX_X))
            link(dve.reduce_sum(f.full_sum[:, :], f.full[:, 0:6], AX_X))
            dve.wait_ge(tallied, 1)
            every = float(P * T * (H0 + H1 + NSEG + 3))
            dve.tensor_scalar(f.flag[0:1, 0:1], m.psum[0][0:1, 0:1], every, None, ALU.not_equal).then_inc(flagged, 1)
            dve.wait_ge(flagged, 1)

        @block.tensor
        def _(pe):
            pe.wait_ge(chain, 4 + H1 + 7)
            pe.matmul(m.psum[0][0:1, 0:1], f.full_sum[:, :], m.ones[:, 0:1], start=True, stop=True).then_inc(tallied, 1)

        @block.sync
        def _(sp):
            sp.wait_ge(added, 1)
            sp.dma_start(out.rearrange("(t p) d -> p t d", p=P), m.x_sb[:, :, :]).then_inc(written, 16)
            sp.wait_ge(written, 16)


def sparse_path(nc, ctx, m, f, x, adj, out):
    load_x(nc, ctx, m, x, "")
    sparse_constants(nc, ctx, m, f)
    transform(nc, ctx, m, 0, "_0")
    publish(nc, ctx, m, f, 0)
    find_and_attend0(nc, ctx, m, f, adj)
    finish0(nc, ctx, m, f)
    transform(nc, ctx, m, 1, "_1")
    publish(nc, ctx, m, f, 1)
    attend1(nc, ctx, m, f)
    finish1(nc, ctx, m, f, out)


def any_path(nc, ctx, m, f, x, adj, out):
    def sb(name, shape, dt=F32):
        return ctx.enter_context(nc.sbuf_tensor(name, shape, dt))

    g = Memory()
    g.adj = f.adj[:, 0, :]
    g.e = f.adj[:, 1, :]
    g.row = f.adj[:, 2, :]
    g.att = f.sums[:, 0:T * D].rearrange("p (t d) -> p t d", t=T)
    g.diag = sb("any_diag", [P, BPC, P])
    g.p_t = sb("any_p_t", [P, 2, CHUNK])
    g.top = sb("any_top", [P, 4])
    load_x(nc, ctx, m, x, "_any")
    for layer in range(2):
        transform(nc, ctx, m, layer, f"_nodes{layer}")
        attend_any(nc, ctx, m, layer, adj, g, f"_any{layer}")
        finish_any(nc, ctx, m, layer, out, g, f"_end{layer}")


def build(nc, x, adj, W0, al, ar, W1, b1, a1, out):
    with ExitStack() as ctx:
        m = allocate(nc, ctx)
        prepare(nc, ctx, m, W0, al, ar, W1, b1, a1)
        f = allocate_sparse(nc, ctx)
        sparse_path(nc, ctx, m, f, x, adj, out)
        failed = nc.values_load(f.flag[0:1, 0:1], min_val=0, max_val=1, skip_runtime_bounds_check_because="0 or 1")
        with nc.If(failed > 0):
            nc.all_engine_barrier()
            any_path(nc, ctx, m, f, x, adj, out)


_INS = ['x', 'adj', 'L0_gnn_W', 'L0_gnn_a_l', 'L0_gnn_a_r', 'L1_gnn_W', 'L1_gnn_b', 'L1_gnn_a']
_OUTS = [((4096, 128), 'float32')]


def kernel(**inputs):
    import numpy as _np
    import concourse.bacc as _bacc
    from concourse import mybir as _mybir
    from concourse.bass_utils import run_bass_kernel_spmd as _run
    nc = _bacc.Bacc("TRN2", target_bir_lowering=False, num_devices=1)
    arrays, args = {}, []
    for name in _INS:
        a = _np.ascontiguousarray(inputs[name])
        arrays[f"in_{name}_dram"] = a
        args.append(nc.dram_tensor(f"in_{name}_dram", a.shape, _mybir.dt.from_np(a.dtype), kind="ExternalInput").ap())
    for i, (shape, dtype) in enumerate(_OUTS):
        dt = _mybir.dt.from_np(_np.dtype(dtype))
        args.append(nc.dram_tensor(f"out_{i}_dram", shape, dt, kind="ExternalOutput").ap())
    build(nc, *args)
    r = _run(nc, [arrays], core_ids=[0])
    return r.results[0]["out_0_dram"]
```

```python
from contextlib import ExitStack

import concourse.bass as bass
from concourse import mybir

F32 = mybir.dt.float32
U32 = mybir.dt.uint32
I32 = mybir.dt.int32
BF16 = mybir.dt.bfloat16
ALU = mybir.AluOpType
ACT = mybir.ActivationFunctionType
AX_X = mybir.AxisListType.X

P = 128
N = 4096
D = 128
T = N // P
H0, H1 = 4, 8
D0, D1 = D // H0, D // H1
S0, S1 = D + 4 * H0, D + 4 * H1
SM = S1
SLOPE = 0.2
EPS = 1e-5
BIG = 1e30
CHUNK = 512
NCH = N // CHUNK
BPC = CHUNK // P

HALF = N // 2
SEG = 512
NSEG = HALF // SEG
FOUND = 8
CAND = NSEG * FOUND
K = 16
EC = 5
E = EC * P
PAIR = 2 * EC - 1
G0, G1 = D + 2 * H0, D + 2 * H1
V0, V1 = D + H0, D + H1
GROUPS = 4
GT = T // GROUPS
HIT = float(N)
DEN_MAX = 1e30


class Memory:
    pass


def allocate(nc, ctx):
    m = Memory()

    def sb(name, shape, dt=F32):
        return ctx.enter_context(nc.sbuf_tensor(name, shape, dt))

    m.ident = sb("ident", [P, P])
    m.ones = sb("ones", [P, P])
    m.head0 = sb("head0", [P, H0])
    m.head1 = sb("head1", [P, H1])
    m.w_in = sb("w_in", [P, 2, D])
    m.a_in = sb("a_in", [P, 5])
    m.spread0 = sb("spread0", [P, 4 * H0])
    m.spread1 = sb("spread1", [P, 4 * H1])
    m.weights0 = sb("weights0", [P, S0])
    m.weights1 = sb("weights1", [P, S1])
    m.bias = sb("bias", [P, S1])
    m.eps = sb("eps", [P, 1])
    m.x_sb = sb("x_sb", [P, T, D])
    m.table = sb("table", [P, T, SM])
    m.stats = sb("stats", [P, T, 6])
    m.mean_var = sb("mean_var", [P, T, 2])
    m.rstd = sb("rstd", [P, T])
    m.shift = sb("shift", [P, T])
    m.normed = sb("normed", [P, 4, D])
    m.h_t = sb("h_t", [P, 4, P])
    m.psum_all = ctx.enter_context(nc.psum_tensor("psum_all", [P, 8 * CHUNK], F32))
    m.shapes = ctx.enter_context(nc.semaphore("shapes"))
    m.weights_done = ctx.enter_context(nc.semaphore("weights_done"))
    m.psum = [m.psum_all[:, b * CHUNK:(b + 1) * CHUNK] for b in range(8)]
    return m


def prepare(nc, ctx, m, block, W0, al, ar, W1, b1, a1):
    def sem(name):
        return ctx.enter_context(nc.semaphore(name))

    w_loaded, shapes, folded, on_pe, evacuated = (
        sem("w_loaded"), m.shapes, sem("folded"), sem("on_pe"), m.weights_done)

    @block.scalar
    def _(act):
        act.dma_start(m.w_in[:, 0, :], W0[:, :]).then_inc(w_loaded, 16)
        act.dma_start(m.w_in[:, 1, :], W1[:, :]).then_inc(w_loaded, 16)
        act.dma_start(m.a_in[:, 0:1], ar.rearrange("h (d o) -> (h d) o", o=1)).then_inc(w_loaded, 16)
        act.dma_start(m.a_in[:, 1:2], al.rearrange("h (d o) -> (h d) o", o=1)).then_inc(w_loaded, 16)
        act.dma_start(m.a_in[:, 4:5], b1.rearrange("(d o) -> d o", o=1)).then_inc(w_loaded, 16)
        for half, col in ((1, 2), (0, 3)):
            act.dma_start(m.a_in[:, col:col + 1],
                          a1[:, half * D1:(half + 1) * D1].rearrange("h (d o) -> h d o", o=1)).then_inc(w_loaded, 16)

    @block.gpsimd
    def _(pool):
        pool.memset(m.ident[:, :], 0.0).then_inc(shapes, 1)
        pool.memset(m.ones[:, :], 1.0).then_inc(shapes, 1)
        pool.memset(m.head0[:, :], 1.0).then_inc(shapes, 1)
        pool.memset(m.head1[:, :], 1.0).then_inc(shapes, 1)
        pool.memset(m.eps[:, :], EPS).then_inc(shapes, 1)
        pool.wait_ge(shapes, 5)
        pool.affine_select(out=m.ident[:, :], in_=m.ident[:, :], compare_op=ALU.not_equal, fill=1.0,
                           base=0, pattern=[[-1, P]], channel_multiplier=1).then_inc(shapes, 1)
        for mask, heads, d in ((m.head0, H0, D0), (m.head1, H1, D1)):
            pool.affine_select(out=mask[:, :], in_=mask[:, :], compare_op=ALU.is_ge, fill=0.0,
                               base=0, pattern=[[-d, heads]], channel_multiplier=1).then_inc(shapes, 1)
        pool.wait_ge(shapes, 8)
        for mask, heads, d in ((m.head0, H0, D0), (m.head1, H1, D1)):
            pool.affine_select(out=mask[:, :], in_=mask[:, :], compare_op=ALU.is_ge, fill=0.0,
                               base=d - 1, pattern=[[d, heads]], channel_multiplier=-1).then_inc(shapes, 1)

    @block.vector
    def _(dve):
        dve.wait_ge(w_loaded, 7 * 16)
        dve.wait_ge(shapes, 10)
        for k in range(2):
            dve.tensor_scalar(m.spread0[:, 2 * k * H0:(2 * k + 1) * H0], m.head0[:, :], m.a_in[:, k:k + 1], None,
                              ALU.mult).then_inc(folded, 1)
            dve.tensor_scalar(m.spread1[:, 2 * k * H1:(2 * k + 1) * H1], m.head1[:, :], m.a_in[:, 2 + k:3 + k],
                              None, ALU.mult).then_inc(folded, 1)
        dve.wait_ge(folded, 4)
        for k in range(2):
            for sp_, h in ((m.spread0, H0), (m.spread1, H1)):
                dve.tensor_scalar(sp_[:, (2 * k + 1) * h:(2 * k + 2) * h], sp_[:, 2 * k * h:(2 * k + 1) * h],
                                  SLOPE, None, ALU.mult).then_inc(folded, 1)
        dve.wait_ge(on_pe, 5)
        dve.tensor_copy(m.weights0[:, 0:D], m.psum[0][:, 0:D]).then_inc(evacuated, 1)
        dve.tensor_copy(m.weights1[:, 0:D], m.psum[1][:, 0:D]).then_inc(evacuated, 1)
        dve.tensor_copy(m.weights0[:, D:S0], m.psum[2][:, 0:4 * H0]).then_inc(evacuated, 1)
        dve.tensor_copy(m.weights1[:, D:S1], m.psum[3][:, 0:4 * H1]).then_inc(evacuated, 1)
        dve.tensor_copy(m.bias[:, :], m.psum[4][:, 0:S1]).then_inc(evacuated, 1)

    @block.tensor
    def _(pe):
        pe.wait_ge(w_loaded, 7 * 16)
        pe.wait_ge(shapes, 10)
        pe.transpose(m.psum[0][:, 0:D], m.w_in[:, 0, :], m.ident[:, :]).then_inc(on_pe, 1)
        pe.transpose(m.psum[1][:, 0:D], m.w_in[:, 1, :], m.ident[:, :]).then_inc(on_pe, 1)
        pe.wait_ge(folded, 8)
        pe.matmul(m.psum[2][:, 0:4 * H0], m.w_in[:, 0, :], m.spread0[:, :], start=True, stop=True).then_inc(on_pe, 1)
        pe.matmul(m.psum[3][:, 0:4 * H1], m.w_in[:, 1, :], m.spread1[:, :], start=True, stop=True).then_inc(on_pe, 1)
        bias = m.a_in[:, 4:5].to_broadcast([P, P])
        pe.matmul(m.psum[4][:, 0:D], bias, m.ident[:, :], start=True, stop=True)
        pe.matmul(m.psum[4][:, D:S1], bias, m.spread1[:, :], start=True, stop=True).then_inc(on_pe, 1)


def load_x(m, block, x, x_loaded):
    count = T // len(x_loaded)

    @block.sync
    def _(sp):
        for g, loaded in enumerate(x_loaded):
            tiles = slice(g * count, (g + 1) * count)
            sp.dma_start(m.x_sb[:, tiles, :], x.rearrange("(t p) d -> p t d", p=P)[:, tiles, :]).then_inc(loaded, 16)


def take_statistics(dve, m, first, count, stats_done, var_done):
    for t in range(first, first + count):
        dve.bn_stats(m.stats[:, t, :], m.x_sb[:, t, :]).then_inc(stats_done, 1)
    for t in range(first, first + count):
        dve.wait_ge(stats_done, t + 1)
        dve.bn_aggr(m.mean_var[:, t, :], m.stats[:, t, :]).then_inc(var_done, 1)


def statistics(nc, ctx, m, block, x_loaded, tag):
    stats_done = ctx.enter_context(nc.semaphore("stats_done" + tag))
    var_done = ctx.enter_context(nc.semaphore("var_done" + tag))

    @block.vector
    def _(dve):
        count = T // len(x_loaded)
        for g, loaded in enumerate(x_loaded):
            dve.wait_ge(loaded, 16)
            take_statistics(dve, m, g * count, count, stats_done, var_done)

    return var_done


def take_roots(nc, ctx, m, block, tag, var_done):
    root_done = ctx.enter_context(nc.semaphore("root_done" + tag))

    @block.scalar
    def _(act):
        act.wait_ge(m.shapes, 10)
        act.wait_ge(var_done, T)
        act.activation(m.rstd[:, :], m.mean_var[:, :, 1], ACT.Sqrt, bias=m.eps[:, 0:1]).then_inc(root_done, 1)

    return root_done


def transform(nc, ctx, m, block, layer, tag, root_done):
    weights, cols = (m.weights0, S0) if layer == 0 else (m.weights1, S1)

    def sem(name):
        return ctx.enter_context(nc.semaphore(name + tag))

    rstd_done, norm_done, odd_norm_done, turned, relu_done, product_done, stored = (
        sem("rstd_done"), sem("norm_done"), sem("odd_norm_done"), sem("turned"),
        sem("relu_done"), sem("product_done"), sem("stored"))

    B = 4

    def rounds(engine, step):
        step(1)
        with engine.Fori(0, (T // B - 2) // 3) as n:
            for k in range(2, 5):
                step(3 * n + k)

    @block.vector
    def _(dve):
        dve.wait_ge(root_done, 1)
        dve.reciprocal(m.rstd[:, :], m.rstd[:, :]).then_inc(rstd_done, 1)
        dve.wait_ge(rstd_done, 1)
        dve.scalar_tensor_tensor(out=m.shift[:, :], in0=m.mean_var[:, :, 0], scalar=-1.0, in1=m.rstd[:, :],
                                 op0=ALU.mult, op1=ALU.mult).then_inc(rstd_done, 1)

        def norm(t, b):
            dve.tensor_scalar(m.normed[:, b, :], m.x_sb[:, bass.ds(t, 1), :], m.mean_var[:, bass.ds(t, 1), 0:1],
                              m.rstd[:, bass.ds(t, 1)], ALU.subtract, ALU.mult).then_inc(norm_done, 1)

        def store(t, b):
            dve.wait_ge(product_done, t + 1)
            to = m.table[:, bass.ds(t, 1), 0:cols]
            if layer == 0:
                dve.tensor_copy(to, m.psum[B + b][:, 0:cols]).then_inc(stored, 1)
            else:
                dve.tensor_tensor(to, m.psum[B + b][:, 0:cols], m.bias[:, :], ALU.add).then_inc(stored, 1)
        for b in range(0, B, 2):
            norm(b, b)

        def step(i):
            for b in range(B):
                if b % 2 == 0:
                    dve.wait_ge(turned, B * (i - 1) + b + 1)
                    norm(B * i + b, b)
                store(B * (i - 1) + b, b)
        rounds(dve, step)
        for b in range(B):
            store(T - B + b, b)

    @block.scalar
    def _(act):
        def relu(t, b):
            act.wait_ge(turned, t + 1)
            act.activation(m.h_t[:, b, :], m.psum[b][:, 0:P], ACT.Relu).then_inc(relu_done, 1)

        def norm(t, b):
            act.activation(m.normed[:, b, :], m.x_sb[:, bass.ds(t, 1), :], ACT.Identity, bias=m.shift[:, bass.ds(t, 1)],
                           scale=m.rstd[:, bass.ds(t, 1)]).then_inc(odd_norm_done, 1)
        act.wait_ge(rstd_done, 2)
        norm(1, 1)
        norm(3, 3)
        for b in range(B):
            relu(b, b)

        def step(i):
            for b in range(1, B, 2):
                act.wait_ge(turned, B * (i - 1) + b + 1)
                norm(B * i + b, b)
            for b in range(B):
                act.wait_ge(product_done, B * (i - 1) + b + 1)
                relu(B * i + b, b)
        rounds(act, step)

    @block.tensor
    def _(pe):
        pe.wait_ge(m.weights_done, 5)

        def turn(t, i, b):
            pe.wait_ge(odd_norm_done if b % 2 else norm_done, B // 2 * i + b // 2 + 1)
            pe.transpose(m.psum[b][:, 0:P], m.normed[:, b, :], m.ident[:, :]).then_inc(turned, 1)

        def product(t, b):
            pe.wait_ge(relu_done, t + 1)
            pe.matmul(m.psum[B + b][:, 0:cols], m.h_t[:, b, :], weights[:, :], start=True,
                      stop=True).then_inc(product_done, 1)
        for b in range(B):
            turn(b, 0, b)
        product(0, 0)
        product(1, 1)

        def step(i):
            for b in range(B):
                turn(B * i + b, i, b)
                if b >= 2 or not isinstance(i, int) or i >= 2:
                    pe.wait_ge(stored, B * i + b - B - 1)
                product(B * i + b - 2, (b + 2) % B)
        rounds(pe, step)
        pe.wait_ge(stored, T - B)
        product(T - 2, B - 2)
        product(T - 1, B - 1)

    return stored


def attend_any(nc, ctx, m, layer, adj, g, tag):
    heads, dh = (H0, D0) if layer == 0 else (H1, D1)

    def sem(name):
        return ctx.enter_context(nc.semaphore(name + tag))

    diag_done, spread_done, row_done, a_loaded, chain, shifted, exp_done, turned, turn_copied, summed, normed = (
        sem("diag_done"), sem("spread_done"), sem("row_done"), sem("a_loaded"), sem("chain"), sem("shifted"),
        sem("exp_done"), sem("turned"), sem("turn_copied"), sem("summed"), sem("normed"))
    STEPS = 7 if layer == 0 else 5

    with nc.Block() as block:
        @block.sync
        def _(sp):
            sp.dma_start(g.adj[:, :], adj[0:P, :]).then_inc(a_loaded, 16)
            with sp.Fori(1, heads * T) as k:
                sp.wait_ge(shifted, k)
                sp.dma_start(g.adj[:, :], adj[bass.ds((k % T) * P, P), :]).then_inc(a_loaded, 16)

        @block.vector
        def _(dve):
            with dve.Fori(0, heads) as h:
                for c in range(NCH):
                    if c:
                        dve.wait_ge(spread_done, h * NCH + c)
                    dve.tensor_tensor(g.diag[:, :, :], m.ident[:, None, :].to_broadcast([P, BPC, P]),
                                      m.table[:, c * BPC:(c + 1) * BPC, bass.ds(D + h, 1)].to_broadcast([P, BPC, P]),
                                      ALU.mult).then_inc(diag_done, 1)
                with dve.Fori(0, T) as i:
                    k = h * T + i
                    at = [0]

                    def step(ins):
                        ins.then_inc(chain, 1)
                        at[0] += 1
                        dve.wait_ge(chain, k * STEPS + at[0])
                    dve.wait_ge(a_loaded, 16 * k + 16)
                    if layer == 0:
                        here = g.adj[:, bass.ds(i * P, P)]
                        step(dve.tensor_tensor(here, here, m.ident[:, :], ALU.add))
                    step(dve.tensor_scalar(g.adj[:, :], g.adj[:, :], 0.0, None,
                                           ALU.is_gt if layer == 0 else ALU.not_equal))
                    dve.wait_ge(row_done, h * NCH + NCH)
                    step(dve.tensor_scalar(g.e[:, :], g.row[:, :],
                                           m.table[:, bass.ds(i, 1), bass.ds(D + 2 * heads + h, 1)], None, ALU.add))
                    step(dve.scalar_tensor_tensor(out=g.e[:, :], in0=g.e[:, :], scalar=SLOPE, in1=g.e[:, :],
                                                  op0=ALU.mult, op1=ALU.max))
                    if layer == 0:
                        step(dve.tensor_scalar(g.adj[:, :], g.adj[:, :], BIG, -BIG, ALU.mult, ALU.add))
                        step(dve.tensor_tensor(g.e[:, :], g.e[:, :], g.adj[:, :], ALU.add))
                    else:
                        step(dve.tensor_tensor(g.e[:, :], g.e[:, :], g.adj[:, :], ALU.mult))
                    step(dve.reduce_max(g.top[:, 0:1], g.e[:, :], AX_X))
                    dve.tensor_scalar(g.top[:, 1:2], g.top[:, 0:1], -1.0, None, ALU.mult).then_inc(shifted, 1)
                    for c in range(NCH):
                        dve.wait_ge(turned, k * NCH + c + 1)
                        if c >= 2:
                            dve.wait_ge(summed, k * NCH + c - 1)
                        dve.tensor_copy(g.p_t[:, c % 2, :], m.psum[c % 2][:, :]).then_inc(turn_copied, 1)
                    dve.wait_ge(summed, k * NCH + NCH)
                    dve.reciprocal(g.top[:, 3:4], g.top[:, 2:3]).then_inc(normed, 1)
                    dve.wait_ge(normed, 2 * k + 1)
                    dve.tensor_scalar(g.att[:, bass.ds(i, 1), bass.ds(h * dh, dh)], m.psum[3][:, 0:dh],
                                      g.top[:, 3:4], None, ALU.mult).then_inc(normed, 1)
                    dve.wait_ge(normed, 2 * k + 2)

        @block.scalar
        def _(act):
            with act.Fori(0, heads) as h:
                for c in range(NCH):
                    act.wait_ge(spread_done, h * NCH + c + 1)
                    act.activation(g.row[:, c * CHUNK:(c + 1) * CHUNK], m.psum[2][:, :], ACT.Copy).then_inc(row_done, 1)
                with act.Fori(0, T) as i:
                    k = h * T + i
                    act.wait_ge(shifted, k + 1)
                    act.activation(g.e[:, :], g.e[:, :], ACT.Exp, bias=g.top[:, 1:2],
                                   accum_out=g.top[:, 2:3]).then_inc(exp_done, 1)

        @block.tensor
        def _(pe):
            with pe.Fori(0, heads) as h:
                for c in range(NCH):
                    pe.wait_ge(diag_done, h * NCH + c + 1)
                    if c:
                        pe.wait_ge(row_done, h * NCH + c)
                    pe.matmul(m.psum[2][:, :], m.ones[:, :], g.diag[:, :, :], start=True, stop=True).then_inc(spread_done, 1)
                with pe.Fori(0, T) as i:
                    k = h * T + i

                    def turn(c):
                        if c >= 2:
                            pe.wait_ge(turn_copied, k * NCH + c - 1)
                        for b in range(BPC):
                            last = pe.transpose(m.psum[c % 2][:, b * P:(b + 1) * P],
                                                g.e[:, c * CHUNK + b * P:c * CHUNK + (b + 1) * P], m.ident[:, :])
                        last.then_inc(turned, 1)
                    pe.wait_ge(exp_done, k + 1)
                    turn(0)
                    for c in range(NCH):
                        if c + 1 < NCH:
                            turn(c + 1)
                        pe.wait_ge(turn_copied, k * NCH + c + 1)
                        for b in range(BPC):
                            blk = c * BPC + b
                            last = pe.matmul(m.psum[3][:, 0:dh], g.p_t[:, c % 2, b * P:(b + 1) * P],
                                             m.table[:, blk, bass.ds(h * dh, dh)], start=blk == 0, stop=blk == T - 1)
                        last.then_inc(summed, 1)


def finish_any(nc, ctx, m, layer, out, g, tag):
    def sem(name):
        return ctx.enter_context(nc.semaphore(name + tag))

    low, exp_done, high, added, written = sem("low"), sem("exp_done"), sem("high"), sem("added"), sem("written")
    flat = g.att[:, :, :].rearrange("p t d -> p (t d)")
    x_flat = m.x_sb[:, :, :].rearrange("p t d -> p (t d)")
    with nc.Block() as block:
        @block.vector
        def _(dve):
            if layer == 0:
                dve.tensor_scalar(g.e[:, :], flat, 0.0, None, ALU.min).then_inc(low, 1)
                dve.tensor_scalar(flat, flat, 0.0, -1.0, ALU.max, ALU.add).then_inc(high, 1)
                dve.wait_ge(high, 1)
                dve.wait_ge(exp_done, 1)
                dve.tensor_tensor(flat, flat, g.e[:, :], ALU.add).then_inc(high, 1)
                dve.wait_ge(high, 2)
            dve.tensor_tensor(x_flat, x_flat, flat, ALU.add).then_inc(added, 1)

        @block.scalar
        def _(act):
            if layer == 0:
                act.wait_ge(low, 1)
                act.activation(g.e[:, :], g.e[:, :], ACT.Exp).then_inc(exp_done, 1)

        @block.sync
        def _(sp):
            if layer == 1:
                sp.wait_ge(added, 1)
                sp.dma_start(out.rearrange("(t p) d -> p t d", p=P), m.x_sb[:, :, :]).then_inc(written, 16)
                sp.wait_ge(written, 16)


def allocate_sparse(nc, ctx):
    f = Memory()

    def sb(name, shape, dt=F32):
        return ctx.enter_context(nc.sbuf_tensor(name, shape, dt))

    f.adj = sb("adj_rows", [P, 3, N])
    f.sign = sb("sign", [P, 2, N], BF16)
    f.hit = sb("hit", [P, 2, P], BF16)
    f.ones_b = sb("ones_b", [64, P], BF16)
    f.column = sb("column", [64, HALF], BF16)
    f.before = sb("before", [P, P])
    f.edge_odd = sb("edge_odd", [P, 2, E])
    f.my_edge = sb("my_edge", [P, 2, EC, K])
    f.slot_no = sb("slot_no", [P, K])
    f.sign_sum = sb("sign_sum", [P, T, 2])
    f.cand = sb("cand", [P, 2, CAND])
    f.found = sb("found", [P, T, CAND])
    f.keys = sb("keys", [P, 2 * CAND])
    f.rest = sb("rest", [P, 2 * CAND])
    f.scrap = sb("scrap", [P, CAND])
    f.scrap2 = sb("scrap2", [P, 2 * CAND])
    f.degree_upper = sb("degree_upper", [P, T])
    f.own = sb("own", [P, T, V0])
    f.ints = f.own[:, :, :].rearrange("p t v -> p (t v)")[:, 0:E + EC * K].bitcast(I32)
    f.diagonal = sb("diagonal", [P, T])
    f.degree = sb("degree", [P, T])
    f.first = sb("first", [P, T])
    f.centre = sb("centre", [P, T])
    f.rows = sb("rows", [P, 2 * K])
    f.rows_b = sb("rows_b", [P, 2, 2 * K], BF16)
    f.score_b = sb("score_b", [P, 3, T, 2 * H1], BF16)
    f.score_r = sb("score_r", [P, T * 2 * H1])
    f.ident_b = sb("ident_b", [P, P], BF16)
    f.row_scores = sb("row_scores", [P, T, 2 * H0])
    f.self_sum = sb("self_sum", [P, T, 2 * H0])
    f.apart = sb("apart", [P, 2, E])
    f.member = sb("member", [P, 2, E], BF16)
    f.member_t = sb("member_t", [P, 4, EC, P])
    f.is_slot = sb("is_slot", [P, EC, K])
    f.slot_val = sb("slot_val", [P, EC, K])
    f.key = sb("key", [P, EC])
    f.index = sb("index", [P, T, EC], U32)
    f.edge_row = sb("edge_row", [P, 4, EC, 2 * H1])
    f.gathered = sb("gathered", [P, 2, PAIR, G1])
    f.pair = sb("pair", [P, EC, 2 * H1])
    f.logit = sb("logit", [P, EC, H1])
    f.value = sb("value", [P, 2, EC, V1])
    f.sums = sb("sums", [P, T * V1])
    f.den0 = sb("den0", [P, T, H0])
    f.rden0 = sb("rden0", [P, T, H0])
    f.den = sb("den", [P, T, H1])
    f.total = sb("total", [P, D])
    f.part = sb("part", [P, D])
    f.rden = sb("rden", [P, H1])
    f.self_w = sb("self_w", [P, T])
    f.full = sb("full", [P, 8])
    f.full_sum = sb("full_sum", [P, 1])
    f.flag = sb("flag", [1, 1], I32)
    f.diagonal_loaded = ctx.enter_context(nc.semaphore("diagonal_loaded"))
    f.filled = ctx.enter_context(nc.semaphore("filled"))
    f.signed = ctx.enter_context(nc.semaphore("signed"))
    f.copied = ctx.enter_context(nc.semaphore("copied"))
    f.t0 = nc.dram_tensor("node_table0", (N, G0), F32).ap()
    f.t1 = nc.dram_tensor("node_table1", (N, G1), F32).ap()
    return f


def one(i):
    return bass.ds(i, 1)


def sparse_constants(nc, ctx, m, f, block):
    def sem(name):
        return ctx.enter_context(nc.semaphore(name))

    filled, copied = f.filled, f.copied
    wide = f.sums[:, 0:HALF].bitcast(I32)
    @block.gpsimd
    def _(pool):
        pool.memset(f.hit[:, :, :], 0.0).then_inc(filled, 1)
        pool.memset(f.ones_b[:, :], 1.0).then_inc(filled, 1)
        pool.memset(f.before[:, :], 1.0).then_inc(filled, 1)
        pool.iota(f.ints[:, 0:E], [[1, E]], base=0, channel_multiplier=0).then_inc(filled, 1)
        pool.memset(f.sums[0:64, 0:HALF], 0.0).then_inc(filled, 1)
        pool.wait_ge(filled, 5)
        pool.iota(wide[0:1, :], [[64, HALF // 64], [0, 64]], base=0, channel_multiplier=0).then_inc(filled, 1)
        pool.wait_ge(filled, 6)
        pool.iota(wide[32:33, :], [[0, HALF // 64], [1, 64]], base=0, channel_multiplier=0).then_inc(filled, 1)
        pool.wait_ge(filled, 7)
        pool.iota(f.ints[:, E:E + EC * K], [[P, EC], [0, K]], base=0, channel_multiplier=1).then_inc(filled, 1)
        pool.wait_ge(filled, 8)
        for k in range(2):
            pool.affine_select(out=f.hit[:, k, :], in_=f.hit[:, k, :], compare_op=ALU.not_equal,
                               fill=float((k + 1) * HALF), base=0, pattern=[[-1, P]],
                               channel_multiplier=1).then_inc(filled, 1)
        pool.affine_select(out=f.before[:, :], in_=f.before[:, :], compare_op=ALU.is_gt, fill=0.0,
                           base=0, pattern=[[1, P]], channel_multiplier=-1).then_inc(filled, 1)

    @block.vector
    def _(dve):
        dve.wait_ge(filled, 11)
        dve.tensor_copy(f.column[:, :], wide[0:64, :]).then_inc(copied, 1)
        dve.tensor_scalar(f.edge_odd[:, 0, :], f.ints[:, 0:E], 2.0, 1.0, ALU.mult, ALU.add).then_inc(copied, 1)
        dve.tensor_scalar(f.edge_odd[:, 1, :], f.ints[:, 0:E], -2.0, 2.0 * E - 1.0, ALU.mult, ALU.add).then_inc(copied, 1)
        dve.tensor_copy(f.slot_no[:, :], f.ints[:, 0:K]).then_inc(copied, 1)
        edge = f.ints[:, E:E + EC * K].rearrange("p (c k) -> p c k", c=EC)
        dve.tensor_copy(f.my_edge[:, 0, :, :], edge).then_inc(copied, 1)
        dve.tensor_scalar(f.my_edge[:, 1, :, :], edge, -1.0, E - 1.0, ALU.mult, ALU.add).then_inc(copied, 1)
        dve.tensor_copy(f.ident_b[:, :], m.ident[:, :]).then_inc(copied, 1)
        dve.wait_ge(copied, 7)


def split(dve, f, scores, width, done):
    part = [f.score_b[:, k, :, 0:width] for k in range(3)]
    left = f.score_r[:, 0:T * width].rearrange("p (t w) -> p t w", t=T)
    dve.tensor_copy(part[0], scores).then_inc(done, 1)
    dve.wait_ge(done, 1)
    dve.tensor_tensor(left, scores, part[0], ALU.subtract).then_inc(done, 1)
    dve.wait_ge(done, 2)
    dve.tensor_copy(part[1], left).then_inc(done, 1)
    dve.wait_ge(done, 3)
    dve.tensor_tensor(part[2], left, part[1], ALU.subtract).then_inc(done, 1)


def own_edges(nc, ctx, m, f, block, stored):
    weight_done, own_done = ctx.enter_context(nc.semaphore("self_weight")), ctx.enter_context(nc.semaphore("own_done"))

    @block.gpsimd
    def _(pool):
        pool.wait_ge(f.diagonal_loaded, 16)
        pool.tensor_scalar(f.self_w[:, :], f.diagonal[:, :], 0.0, None, ALU.is_le).then_inc(weight_done, 1)
        pool.wait_ge(weight_done, 1)
        for g in range(GROUPS):
            tiles = slice(g * GT, (g + 1) * GT)
            weights = f.self_w[:, tiles][:, :, None]
            pool.wait_ge(stored, (g + 1) * GT)
            pool.tensor_tensor(f.own[:, tiles, 0:D], m.table[:, tiles, 0:D], weights.to_broadcast([P, GT, D]),
                               ALU.mult).then_inc(own_done, 1)
            pool.tensor_copy(f.own[:, tiles, D:V0], weights.to_broadcast([P, GT, H0])).then_inc(own_done, 1)

    return own_done


def publish(nc, ctx, m, f, block, layer, stored):
    def sem(name):
        return ctx.enter_context(nc.semaphore(f"{name}_publish{layer}"))

    sent, made, parts_done = sem("sent"), sem("made"), sem("parts_done")
    dest, cols = (f.t0, G0) if layer == 0 else (f.t1, G1)
    to = dest.rearrange("(t p) c -> p t c", p=P)

    @block.sync
    def _(sp):
        for g in range(GROUPS):
            sp.wait_ge(stored, (g + 1) * GT)
            sp.dma_start(to[:, g * GT:(g + 1) * GT, :], m.table[:, g * GT:(g + 1) * GT, 0:cols]).then_inc(sent, 16)

    @block.vector
    def _(dve):
        dve.wait_ge(stored, T)
        if layer == 0:
            dve.tensor_tensor(f.self_sum[:, :, :], m.table[:, :, D:D + 2 * H0], m.table[:, :, D + 2 * H0:S0],
                              ALU.add).then_inc(made, 1)
            dve.wait_ge(made, 1)
            dve.tensor_tensor(f.self_sum[:, :, 0:H0], f.self_sum[:, :, 0:H0], f.self_sum[:, :, H0:2 * H0],
                              ALU.max).then_inc(made, 1)
            dve.wait_ge(made, 2)
            for half in range(2):
                dve.tensor_tensor(f.row_scores[:, :, half * H0:(half + 1) * H0],
                                  m.table[:, :, D + (2 + half) * H0:D + (3 + half) * H0],
                                  f.self_sum[:, :, 0:H0], ALU.subtract).then_inc(made, 1)
            dve.wait_ge(made, 4)
            split(dve, f, f.row_scores[:, :, :], 2 * H0, parts_done)
        else:
            split(dve, f, m.table[:, :, D + 2 * H1:S1], 2 * H1, parts_done)

    return sent, parts_done


def chunks_of(f, r):
    first = (EC - 1) * (r % 2)
    return f.gathered[:, r // 2, first:first + EC, :]


def arrived(r, rounds):
    return 16 * (EC - r % 2) * rounds


def take_signs(act, f, i, u, half):
    cols = slice(half * HALF, (half + 1) * HALF)
    act.activation(f.sign[:, u, cols], f.adj[:, u, cols], ACT.Sign,
                   accum_out=f.sign_sum[:, one(i), half:half + 1]).then_inc(f.signed, 1)


def sign_first(f, block, a_loaded):
    @block.scalar
    def _(act):
        act.wait_ge(a_loaded[0], 16)
        for half in range(2):
            take_signs(act, f, 0, 0, half)


def finish0(nc, ctx, m, f):
    def sem(name):
        return ctx.enter_context(nc.semaphore(name + "_finish0"))

    den_done, rden_done, scaled, low, exp_done, positive, x_done, stats_done = (
        sem("den_done"), sem("rden_done"), sem("scaled"), sem("low"), sem("exp_done"), sem("positive"), sem("x_done"),
        sem("stats_done"))
    sums = f.sums[:, 0:T * V0].rearrange("p (t v) -> p t v", t=T)
    part = f.adj[:, 0, :].rearrange("p (t d) -> p t d", t=T)
    neg = f.adj[:, 1, :].rearrange("p (t d) -> p t d", t=T)
    p = Memory()
    p.var_done = sem("var_done")

    def group(x, g):
        return x[:, g * GT:(g + 1) * GT, :]

    def by_head(x, g):
        return group(x, g).rearrange("p t (h d) -> p t h d", h=H0)

    def invert(dve, g, stored):
        dve.wait_ge(stored, (g + 1) * GT)
        dve.tensor_copy(group(f.den0, g), group(sums[:, :, D:V0], g)).then_inc(den_done, 1)
        dve.reciprocal(group(f.rden0, g), group(sums[:, :, D:V0], g)).then_inc(rden_done, 1)

    def scale(engine, g):
        engine.wait_ge(f.signed, 2 * T)
        engine.wait_ge(rden_done, g + 1)
        engine.tensor_tensor(by_head(part, g), by_head(sums[:, :, 0:D], g),
                             f.rden0[:, g * GT:(g + 1) * GT, :, None].to_broadcast([P, GT, H0, D0]),
                             ALU.mult).then_inc(scaled, 1)

    def low_part(act, g):
        act.wait_ge(scaled, g + 1)
        act.activation(group(neg, g), group(part, g), ACT.Relu, scale=-1.0).then_inc(low, 1)
        act.wait_ge(low, g + 1)
        act.activation(group(neg, g), group(neg, g), ACT.Exp, scale=-1.0).then_inc(exp_done, 1)

    def add_positive(dve, g):
        dve.wait_ge(scaled, g + 1)
        dve.scalar_tensor_tensor(out=group(m.x_sb, g), in0=group(part, g), scalar=0.0, in1=group(m.x_sb, g),
                                 op0=ALU.max, op1=ALU.add).then_inc(positive, 1)

    def close(dve, g):
        dve.wait_ge(positive, g + 1)
        dve.wait_ge(exp_done, g + 1)
        dve.scalar_tensor_tensor(out=group(m.x_sb, g), in0=group(neg, g), scalar=-1.0, in1=group(m.x_sb, g),
                                 op0=ALU.add, op1=ALU.add).then_inc(x_done, 1)
        dve.wait_ge(x_done, g + 1)
        take_statistics(dve, m, g * GT, GT, stats_done, p.var_done)

    p.invert, p.scale, p.low_part, p.add_positive, p.close = invert, scale, low_part, add_positive, close
    p.den_done = den_done
    return p


def find_and_attend0(nc, ctx, m, f, block, adj, a_loaded, table_stored, sent, parts_done, own_done, finish):
    def sem(name):
        return ctx.enter_context(nc.semaphore(name))

    signed, keyed, searched = f.signed, sem("keyed"), sem("searched")
    counted, ranked, placed, bounded, apart_done = (
        sem("counted"), sem("ranked"), sem("placed"), sem("bounded"), sem("apart_done"))
    member_done, spread, turned, member_t_done = sem("member_done"), sem("spread"), sem("turned_edges"), sem("member_t_done")
    picking, indexed, row_copied = sem("picking"), sem("indexed"), sem("row_copied")
    gathered = [sem(f"gathered{r}") for r in range(4)]
    paired, logits_done, weighed, valued, summed, stored = (
        sem("paired"), sem("logits_done"), sem("weighed"), sem("valued"), sem("summed"), sem("sums_stored"))

    kept, passed, shown, parted, opened = sem("kept"), sem("passed"), sem("shown"), sem("parted"), sem("opened")
    key_bank = m.psum[0:NSEG]
    place_ps = m.psum[4][:, 0:1]
    spread_ps = m.psum[5][:, 0:EC * 40].rearrange("p (c k) -> p c k", c=EC)
    turn_ps = m.psum[6][:, 0:EC * P // 2].bitcast(BF16)
    sum_ps = m.psum[7][:, 0:V0]
    W = 2 * K + 2 * H0

    def steps(engine, step):
        for i in range(9):
            step(i, i % 2, i // 4, i % 4, i < T, i >= 1, i >= 4)
        with engine.Fori(1, (T - 8) // 8) as n:
            for k in range(1, 9):
                step(8 * n + k, k % 2, 2 * n + k // 4, k % 4, True, True, True)
        for i in range(T - 7, T + 4):
            step(i, i % 2, i // 4, i % 4, i < T, i - 1 < T, True)

    def past(i, n):
        return not isinstance(i, int) or i >= n

    @block.sync
    def _(sp):
        def load(i, u):
            sp.dma_start(f.adj[:, u, :], adj[bass.ds(i * P, P), :]).then_inc(a_loaded[u], 16)
        with sp.Fori(1, T // 2) as j:
            for u in range(2):
                sp.wait_ge(signed, 2 * (2 * j + u - 1))
                load(2 * j + u, u)

    @block.scalar
    def _(act):
        def sign(i, u, loads, half):
            if half == 0:
                act.wait_ge(a_loaded[u], 16 * loads)
                if past(i, 2):
                    act.wait_ge(keyed, NSEG * (i - 1))
            take_signs(act, f, i, u, half)

        def step(i, u, q, r, search, pack, attend):
            more = not isinstance(i, int) or i + 1 < T
            v = 1 - u
            if pack:
                act.wait_ge(bounded, 2 * i)
                if past(i, 3):
                    act.wait_ge(member_done, i - 2)
                act.activation(f.apart[:, v, :], f.edge_odd[:, v, :], ACT.Abs,
                               bias=f.centre[:, one(i - 1)]).then_inc(apart_done, 1)
            if attend:
                act.wait_ge(logits_done, i - 3)
                if past(i, 6):
                    act.wait_ge(summed, i - 5)
                act.activation(f.value[:, u, :, D:V0], f.logit[:, :, 0:H0], ACT.Exp).then_inc(weighed, 1)
            if more:
                sign(i + 1, v, 2 * q + (r + 1) // 2 + 1, 0)
            if more:
                sign(i + 1, v, 2 * q + (r + 1) // 2 + 1, 1)
            if pack:
                act.wait_ge(turned, i)
                if past(i, 5):
                    act.wait_ge(summed, i - 4)
                act.activation(f.member_t[:, (r - 1) % 4, :, :], turn_ps, ACT.Copy).then_inc(member_t_done, 1)
            if attend and past(i, 5):
                store(i - 5)
            if isinstance(i, int) and i == T + 1:
                finish.low_part(act, 0)

        def store(t):
            act.wait_ge(summed, t + 1)
            act.activation(f.sums[:, bass.ds(t * V0, V0)], sum_ps, ACT.Copy).then_inc(stored, 1)
        steps(act, step)
        finish.low_part(act, 1)
        store(T - 1)
        finish.low_part(act, 2)
        finish.low_part(act, 3)

    @block.tensor
    def _(pe):
        def keys(i, u, seg):
            pe.wait_ge(signed, 2 * i + 2)
            if past(i, 1):
                pe.wait_ge(searched, NSEG * (i - 1) + seg + 1)
            for k in range(2):
                pe.matmul(key_bank[seg], f.hit[:, k, :],
                          f.sign[:, u, k * HALF + seg * SEG:k * HALF + (seg + 1) * SEG], start=k == 0, stop=False)
            pe.matmul(key_bank[seg], f.ones_b[:, :], f.column[:, seg * SEG:(seg + 1) * SEG], start=False,
                      stop=True).then_inc(keyed, 1)

        pe.wait_ge(f.filled, 11)
        pe.wait_ge(f.copied, 7)
        pe.wait_ge(table_stored, T)

        def step(i, u, q, r, search, pack, attend):
            more = not isinstance(i, int) or i + 1 < T
            v = 1 - u
            if pack:
                pe.wait_ge(member_done, i)
                pe.wait_ge(parted, 2 * i)
                if not past(i, 2):
                    pe.wait_ge(parts_done, 4)
                if past(i, 2):
                    pe.wait_ge(row_copied, i - 1)
                    pe.wait_ge(member_t_done, i - 1)
                for c in range(EC):
                    edges = f.member[:, v, c * P:(c + 1) * P]
                    for k in range(2):
                        pe.matmul(spread_ps[:, c, 0:2 * K], edges, f.rows_b[:, k, :], start=k == 0, stop=k == 1)
                    for k in range(3):
                        last = pe.matmul(spread_ps[:, c, 2 * K:W], edges, f.score_b[:, k, one(i - 1), 0:2 * H0],
                                         start=k == 0, stop=k == 2)
                last.then_inc(spread, 1)
                for c in range(EC):
                    last = pe.transpose(turn_ps[:, c * P:(c + 1) * P], f.member[:, v, c * P:(c + 1) * P],
                                        f.ident_b[:, :])
                last.then_inc(turned, 1)
            if search:
                pe.wait_ge(counted, i + 1)
                if past(i, 1):
                    pe.wait_ge(bounded, 2 * i)
                pe.matmul(place_ps, f.before[:, :], f.degree[:, one(i)], start=True, stop=True).then_inc(placed, 1)
            if search and more:
                for seg in range(NSEG):
                    keys(i + 1, v, seg)
            if attend:
                pe.wait_ge(valued, i - 3)
                pe.wait_ge(weighed, i - 3)
                pe.wait_ge(member_t_done, i - 3)
                if past(i, 5):
                    pe.wait_ge(stored, i - 4)
                else:
                    pe.wait_ge(own_done, 2 * GROUPS)
                pe.matmul(sum_ps, m.ident[:, :], f.own[:, one(i - 4), :], start=True, stop=False)
                for c in range(EC):
                    last = pe.matmul(sum_ps, f.member_t[:, r, c, :], f.value[:, u, c, 0:V0],
                                     start=False, stop=c == EC - 1)
                last.then_inc(summed, 1)
        for seg in range(NSEG):
            keys(0, 0, seg)
        steps(pe, step)

    @block.vector
    def _(dve):
        def wait_apart(semaphore, value):
            dve.wait_ge(semaphore, value)
            if not isinstance(value, int):
                dve.sem_inc(passed, 1)

        def search(i, u, seg):
            if past(i, 2) and seg == 0:
                wait_apart(kept, i - 1)
            wait_apart(keyed, NSEG * i + seg + 1)
            dve.max(f.cand[:, u, seg * FOUND:(seg + 1) * FOUND], key_bank[seg]).then_inc(searched, 1)

        def pick_and_rank(i, u, q, r, do_pick, do_rank):
            pairs, row = f.cand[:, u, :], f.keys[:, :]
            if do_rank:
                dve.wait_ge(searched, NSEG * (i + 1))
                dve.tensor_scalar(f.scrap[:, 0:CAND], pairs, 3.0 * HALF, float(HALF), ALU.is_lt, ALU.mult).then_inc(opened, 1)
                dve.tensor_scalar(f.keys[:, CAND:2 * CAND], pairs, float(-HALF), None, ALU.add).then_inc(opened, 1)
                dve.wait_ge(opened, 3 * i + 1)
                dve.tensor_tensor(f.keys[:, 0:CAND], pairs, f.scrap[:, 0:CAND], ALU.add).then_inc(opened, 1)
                if past(i, 1):
                    dve.wait_ge(spread, i)
                dve.wait_ge(opened, 3 * i + 3)
                dve.tensor_scalar(f.scrap2[:, :], row, HIT, 0.0, ALU.is_ge, ALU.add,
                                  accum_out=f.degree[:, one(i)]).then_inc(counted, 1)
            if do_pick:
                dve.wait_ge(spread, i)
                dve.tensor_tensor(f.is_slot[:, :, :], f.my_edge[:, 1 - u, :, :], spread_ps[:, :, K:2 * K],
                                  ALU.is_equal).then_inc(picking, 1)
            if do_rank:
                dve.max(f.rows[:, 0:FOUND], row).then_inc(ranked, 1)
            if do_pick:
                dve.wait_ge(picking, 3 * (i - 1) + 1)
                dve.tensor_tensor(f.slot_val[:, :, :], f.is_slot[:, :, :], spread_ps[:, :, 0:K],
                                  ALU.mult).then_inc(picking, 1)
            if do_rank:
                wait_apart(ranked, 3 * i + 1)
                dve.match_replace(f.rest[:, :], f.rows[:, 0:FOUND], row, 0.0).then_inc(ranked, 1)
            if do_pick:
                dve.wait_ge(picking, 3 * (i - 1) + 2)
                dve.reduce_sum(f.key[:, :], f.slot_val[:, :, :], AX_X).then_inc(picking, 1)
            if do_rank:
                wait_apart(ranked, 3 * i + 2)
                dve.max(f.rows[:, FOUND:K], f.rest[:, :]).then_inc(ranked, 1)
            if do_pick:
                dve.wait_ge(picking, 3 * (i - 1) + 3)
                dve.tensor_scalar(f.index[:, one(i - 1), :], f.key[:, :], -HIT, 0.0, ALU.add, ALU.max).then_inc(indexed, 1)
            if do_rank:
                dve.tensor_copy(f.found[:, one(i), :], pairs).then_inc(kept, 1)
            if do_pick and u == 0:
                dve.wait_ge(indexed, 3 * (2 * q + r // 2) - 1)
                dve.tensor_tensor(f.index[:, one(i - 1), 0:1], f.index[:, one(i - 1), 0:1],
                                  f.index[:, one(i - 2), EC - 1:EC], ALU.max).then_inc(indexed, 1)
            if do_pick:
                dve.tensor_copy(f.edge_row[:, (r - 1) % 4, :, 0:2 * H0], spread_ps[:, :, 2 * K:W]).then_inc(row_copied, 1)

        def begin(g):
            finish.invert(dve, g, stored)
            finish.scale(dve, g)
            finish.add_positive(dve, g)

        def step(i, u, q, r, do_search, pack, attend):
            v = 1 - u
            if pack:
                dve.wait_ge(placed, i)
                dve.wait_ge(counted, i)
                dve.tensor_copy(f.first[:, one(i - 1)], place_ps).then_inc(bounded, 1)
                dve.scalar_tensor_tensor(out=f.centre[:, one(i - 1)], in0=place_ps, scalar=-2.0,
                                         in1=f.degree[:, one(i - 1)], op0=ALU.mult, op1=ALU.subtract).then_inc(bounded, 1)
            if attend:
                dve.wait_ge(gathered[r], arrived(r, q))
                dve.wait_ge(row_copied, i - 3)
                if past(i, 5):
                    dve.wait_ge(weighed, i - 4)
                    dve.wait_ge(logits_done, i - 4)
                dve.tensor_tensor(f.pair[:, :, 0:2 * H0], chunks_of(f, r)[:, :, D:G0], f.edge_row[:, r, :, 0:2 * H0],
                                  ALU.add).then_inc(paired, 1)
                dve.wait_ge(paired, i - 3)
                dve.tensor_tensor(f.logit[:, :, 0:H0], f.pair[:, :, 0:H0], f.pair[:, :, H0:2 * H0],
                                  ALU.max).then_inc(logits_done, 1)
            if pack:
                dve.wait_ge(bounded, 2 * i)
                dve.tensor_scalar(f.rows[:, K:2 * K], f.slot_no[:, :], f.first[:, one(i - 1)], None,
                                  ALU.add).then_inc(shown, 1)
            if do_search:
                search(i, u, 0)
            if do_search:
                search(i, u, 1)
            if pack:
                dve.wait_ge(shown, i)
                dve.wait_ge(ranked, 3 * i)
                dve.tensor_copy(f.rows_b[:, 0, :], f.rows[:, :]).then_inc(parted, 1)
            if pack:
                dve.wait_ge(apart_done, i)
                if past(i, 3):
                    dve.wait_ge(turned, i - 2)
                dve.tensor_scalar(f.member[:, v, :], f.apart[:, v, :], f.degree[:, one(i - 1)], None,
                                  ALU.is_lt).then_inc(member_done, 1)
            if pack:
                dve.wait_ge(parted, 2 * i - 1)
                dve.tensor_tensor(f.rows_b[:, 1, :], f.rows[:, :], f.rows_b[:, 0, :], ALU.subtract).then_inc(parted, 1)
            if do_search:
                search(i, u, 2)
            if do_search:
                search(i, u, 3)
            pick_and_rank(i, u, q, r, pack, do_search)
            if isinstance(i, int) and i == T + 1:
                begin(0)
            if isinstance(i, int) and i == T + 2:
                finish.close(dve, 0)
        steps(dve, step)
        begin(1)
        finish.invert(dve, 2, stored)
        finish.close(dve, 1)
        finish.add_positive(dve, 2)
        finish.invert(dve, 3, stored)
        finish.close(dve, 2)
        finish.add_positive(dve, 3)
        finish.close(dve, 3)
        dve.wait_ge(finish.den_done, GROUPS)

    @block.gpsimd
    def _(pool):
        def weigh(t, v):
            pool.wait_ge(weighed, t + 1)
            if t >= 2:
                pool.wait_ge(summed, t - 1)
            pool.tensor_tensor(
                f.value[:, v, :, 0:D].rearrange("p c (h d) -> p c h d", h=H0),
                chunks_of(f, t % 4)[:, :, 0:D].rearrange("p c (h d) -> p c h d", h=H0),
                f.value[:, v, :, D:V0][:, :, :, None].to_broadcast([P, EC, H0, D0]),
                ALU.mult).then_inc(valued, 1)

        def gather(t, c, where):
            pool.indirect_dma_start(out=f.gathered[:, t % 4 // 2, where, 0:G0], out_offset=None, in_=f.t0[:, :],
                                    in_offset=bass.IndirectOffsetOnAxis(ap=f.index[:, t, c:c + 1], axis=0)
                                    ).then_inc(gathered[(t - 1) % 4 if where == EC - 1 else t % 4], 16)
        pool.wait_ge(sent, 16 * GROUPS)
        for t in range(T + 3):
            if t >= 3:
                weigh(t - 3, (t - 3) % 2)
            if t < T:
                second = t % 2
                pool.wait_ge(indexed, 3 * (t // 2) + (3 if second else 1))
                if t >= 4:
                    pool.wait_ge(valued, t // 2 * 2 - 2)
                for c in range(EC if second else EC - 1):
                    gather(t, c, c + (EC - 1) * second)
        for g in (2, 3):
            finish.scale(pool, g)


def attend1(nc, ctx, m, f, block, sent, parts_done, out, check_edges):
    def sem(name):
        return ctx.enter_context(nc.semaphore(name + "_l1"))

    apart_done, member_done, spread, turned, member_t_done, row_copied = (
        sem("apart_done"), sem("member_done"), sem("spread"), sem("turned"), sem("member_t_done"), sem("row_copied"))
    gathered = [sem(f"gathered{r}") for r in range(4)]
    paired, logits_done, weighed, less_one, valued, summed, stored = (
        sem("paired"), sem("logits_done"), sem("weighed"), sem("less_one"), sem("valued"), sem("summed"), sem("stored"))
    totalled, total_done, finishing, x_done, written = (
        sem("totalled"), sem("total_done"), sem("finishing"), sem("x_done"), sem("written"))
    spread_ps = m.psum[5][:, 0:EC * 2 * H1].rearrange("p (c k) -> p c k", c=EC)
    turn_ps = m.psum[6][:, 0:EC * P // 2].bitcast(BF16)
    sum_ps = [m.psum[7][:, 0:V1], m.psum[1][:, 0:V1]]
    total_ps = m.psum[0][:, :]

    def steps(engine, step):
        for i in range(5):
            step(i, i % 2, i // 4, i % 4, True, i >= 1)
        with engine.Fori(1, T // 4 - 1) as n:
            for k in range(1, 5):
                step(4 * n + k, k % 2, n + k // 4, k % 4, True, True)
        for i in range(T - 3, T + 2):
            step(i, i % 2, i // 4, i % 4, i < T, i <= T)

    def past(i, n):
        return not isinstance(i, int) or i >= n

    @block.scalar
    def _(act):
        def lead(i, u):
            if past(i, 2):
                act.wait_ge(member_done, i - 1)
            act.activation(f.apart[:, u, :], f.edge_odd[:, u, :], ACT.Abs,
                           bias=f.centre[:, one(i)]).then_inc(apart_done, 1)

        def step(i, u, q, r, pack, attend):
            v = 1 - u
            if attend:
                act.wait_ge(logits_done, i)
                if past(i, 2):
                    act.wait_ge(less_one, i - 1)
                act.activation(f.pair[:, :, 0:H1], f.logit[:, :, :], ACT.Exp).then_inc(weighed, 1)
            if pack and (not isinstance(i, int) or i + 1 < T):
                lead(i + 1, v)
            if pack:
                act.wait_ge(turned, i + 1)
                if past(i, 2):
                    act.wait_ge(summed, i - 1)
                act.activation(f.member_t[:, u, :, :], turn_ps, ACT.Copy).then_inc(member_t_done, 1)
        lead(0, 0)
        steps(act, step)

    @block.sync
    def _(sp):
        to = out.rearrange("(t p) d -> p t d", p=P)
        for g in range(GROUPS):
            sp.wait_ge(x_done, (g + 1) * GT)
            sp.dma_start(to[:, g * GT:(g + 1) * GT, :], m.x_sb[:, g * GT:(g + 1) * GT, :]).then_inc(written, 16)
        sp.wait_ge(written, 16 * GROUPS)

    @block.tensor
    def _(pe):
        pe.wait_ge(parts_done, 4)

        def step(i, u, q, r, pack, attend):
            v = 1 - u
            if pack:
                pe.wait_ge(member_done, i + 1)
                if past(i, 1):
                    pe.wait_ge(row_copied, i)
                    pe.wait_ge(member_t_done, i)
                for c in range(EC):
                    for k in range(3):
                        last = pe.matmul(spread_ps[:, c, :], f.member[:, u, c * P:(c + 1) * P],
                                         f.score_b[:, k, one(i), :], start=k == 0, stop=k == 2)
                last.then_inc(spread, 1)
                for c in range(EC):
                    last = pe.transpose(turn_ps[:, c * P:(c + 1) * P], f.member[:, u, c * P:(c + 1) * P],
                                        f.ident_b[:, :])
                last.then_inc(turned, 1)
            if isinstance(i, int) and i == 2:
                for c in range(NCH):
                    last = pe.matmul(total_ps, m.ones[:, :], m.table[:, c * BPC:(c + 1) * BPC, 0:D],
                                     start=c == 0, stop=c == NCH - 1)
                last.then_inc(totalled, 1)
            if attend:
                pe.wait_ge(valued, i)
                pe.wait_ge(member_t_done, i)
                if past(i, 3):
                    pe.wait_ge(finishing, 4 * (i - 2))
                for c in range(EC):
                    last = pe.matmul(sum_ps[v], f.member_t[:, v, c, :], f.value[:, v, c, :], start=c == 0, stop=c == EC - 1)
                last.then_inc(summed, 1)
        steps(pe, step)

    @block.vector
    def _(dve):
        def finish(t, u, i):
            if isinstance(i, int) and i == 2:
                dve.wait_ge(totalled, 1)
                dve.reduce_sum(f.total[:, :], total_ps.rearrange("p (b d) -> p d b", b=BPC), AX_X).then_inc(total_done, 1)
                dve.wait_ge(total_done, 1)
            dve.wait_ge(summed, t + 1)
            dve.tensor_scalar(f.den[:, one(t), :], sum_ps[u][:, D:V1], float(N), None, ALU.add).then_inc(finishing, 1)
            if t is not None and past(i, 3):
                dve.wait_ge(x_done, t)
            dve.wait_ge(finishing, 4 * t + 1)
            dve.tensor_tensor(f.part[:, :], sum_ps[u][:, 0:D], f.total[:, :], ALU.add).then_inc(finishing, 1)
            dve.reciprocal(f.rden[:, :], f.den[:, one(t), :]).then_inc(finishing, 1)
            dve.wait_ge(finishing, 4 * t + 3)
            dve.tensor_tensor(f.part[:, :].rearrange("p (h d) -> p h d", h=H1),
                              f.part[:, :].rearrange("p (h d) -> p h d", h=H1),
                              f.rden[:, :, None].to_broadcast([P, H1, D1]), ALU.mult).then_inc(finishing, 1)
            dve.wait_ge(finishing, 4 * t + 4)
            dve.tensor_tensor(m.x_sb[:, one(t), :], m.x_sb[:, one(t), :], f.part[:, :][:, None, :], ALU.add).then_inc(x_done, 1)

        def step(i, u, q, r, pack, attend):
            v = 1 - u
            if attend:
                before = (r - 1) % 4
                dve.wait_ge(gathered[before], arrived(before, q + (1 if r else 0)))
                dve.wait_ge(row_copied, i)
                if past(i, 2):
                    dve.wait_ge(less_one, i - 1)
                dve.tensor_tensor(f.value[:, v, :, 0:2 * H1], chunks_of(f, before)[:, :, D:G1], f.edge_row[:, v, :, :],
                                  ALU.add).then_inc(paired, 1)
                dve.wait_ge(paired, i)
                dve.tensor_tensor(f.logit[:, :, :], f.value[:, v, :, 0:H1], f.value[:, v, :, H1:2 * H1],
                                  ALU.max).then_inc(logits_done, 1)
            if pack:
                dve.wait_ge(apart_done, i + 1)
                if past(i, 2):
                    dve.wait_ge(turned, i - 1)
                dve.tensor_scalar(f.member[:, u, :], f.apart[:, u, :], f.degree[:, one(i)], None,
                                  ALU.is_lt).then_inc(member_done, 1)
            if attend:
                dve.wait_ge(weighed, i)
                dve.wait_ge(logits_done, i)
                if past(i, 3):
                    dve.wait_ge(summed, i - 2)
                dve.tensor_scalar(f.value[:, v, :, D:V1], f.pair[:, :, 0:H1], 1.0, None, ALU.subtract).then_inc(less_one, 1)
                dve.wait_ge(less_one, i)
                dve.tensor_tensor(
                    f.value[:, v, :, 0:D].rearrange("p c (h d) -> p c h d", h=H1),
                    chunks_of(f, before)[:, :, 0:D].rearrange("p c (h d) -> p c h d", h=H1),
                    f.value[:, v, :, D:V1][:, :, :, None].to_broadcast([P, EC, H1, D1]),
                    ALU.mult).then_inc(valued, 1)
            if pack:
                dve.wait_ge(spread, i + 1)
                dve.tensor_copy(f.edge_row[:, u, :, :], spread_ps).then_inc(row_copied, 1)
            if past(i, 3) or (isinstance(i, int) and i == 2):
                finish(i - 2, u, i)
            if isinstance(i, int) and i == 0:
                check_edges(dve)
        steps(dve, step)

    @block.gpsimd
    def _(pool):
        pool.wait_ge(sent, 16 * GROUPS)
        for t in range(T):
            if t >= 4:
                pool.wait_ge(valued, t // 2 * 2 - 2)
            second = t % 2
            for c in range(second, EC):
                of, col = (t + 1, 0) if not second and c == EC - 1 else (t, c)
                pool.indirect_dma_start(out=f.gathered[:, t % 4 // 2, c + (EC - 1) * second, 0:G1], out_offset=None,
                                        in_=f.t1[:, :],
                                        in_offset=bass.IndirectOffsetOnAxis(ap=f.index[:, of, col:col + 1], axis=0)
                                        ).then_inc(gathered[t % 4], 16)

    return x_done


def checks(nc, ctx, m, f):
    def sem(name):
        return ctx.enter_context(nc.semaphore(name))

    chain, tallied, flagged = sem("check_chain"), sem("tallied"), sem("flagged")
    scrap = f.adj[:, 1, :]
    LINKS = 16
    at = [0]

    def link(dve, ins):
        at[0] += 1
        ins.then_inc(chain, 1)
        dve.wait_ge(chain, at[0])

    def check_edges(dve):
        link(dve, dve.tensor_scalar(scrap[:, 0:T * H0].rearrange("p (t h) -> p t h", t=T), f.den0[:, :, :], DEN_MAX, 0.0,
                                    ALU.is_le, ALU.add, accum_out=f.full[:, 0:1]))
        last_found = f.found[:, :, :].rearrange("p t (s k) -> p (t s) k", k=FOUND)[:, :, FOUND - 1]
        link(dve, dve.tensor_scalar(scrap[:, 0:T * NSEG], last_found, float(HALF), 0.0,
                                    ALU.is_lt, ALU.add, accum_out=f.full[:, 2:3]))
        link(dve, dve.tensor_scalar(scrap[:, 0:T], f.degree[:, :], float(K), 0.0, ALU.is_le, ALU.add,
                                    accum_out=f.full[:, 3:4]))
        link(dve, dve.tensor_tensor(scrap[:, 0:T], f.degree[:, :], f.centre[:, :], ALU.subtract))
        link(dve, dve.tensor_tensor(scrap[:, 0:T], scrap[:, 0:T], f.degree[:, :], ALU.add))
        link(dve, dve.tensor_scalar(scrap[:, T:2 * T], scrap[:, 0:T], 2.0 * E, 0.0, ALU.is_le, ALU.add,
                                    accum_out=f.full[:, 4:5]))
        two = scrap[:, 0:T].rearrange("p (t two) -> p t two", two=2)
        link(dve, dve.tensor_tensor(scrap[:, 2 * T:2 * T + T // 2], two[:, :, 0], two[:, :, 1], ALU.add))
        link(dve, dve.tensor_scalar(scrap[:, 3 * T:3 * T + T // 2], scrap[:, 2 * T:2 * T + T // 2], 2.0 * PAIR * P, 0.0,
                                    ALU.is_le, ALU.add, accum_out=f.full[:, 6:7]))
        hits = scrap[:, 4 * T:(4 + CAND) * T].rearrange("p (t k) -> p t k", t=T)
        link(dve, dve.tensor_scalar(hits, f.found[:, :, :], 2.0 * HALF, None, ALU.is_ge))
        link(dve, dve.reduce_sum(f.degree_upper[:, :], hits, AX_X))
        link(dve, dve.tensor_tensor(scrap[:, 0:T], f.degree[:, :], f.degree_upper[:, :], ALU.subtract))
        link(dve, dve.tensor_tensor(scrap[:, 0:T], scrap[:, 0:T], f.sign_sum[:, :, 0], ALU.is_equal))
        link(dve, dve.tensor_tensor(scrap[:, T:2 * T], f.degree_upper[:, :], f.sign_sum[:, :, 1], ALU.is_equal))
        link(dve, dve.reduce_sum(f.full[:, 5:6], scrap[:, 0:2 * T], AX_X))

    def check_all(block, x_done):
        @block.vector
        def _(dve):
            dve.wait_ge(x_done, T)
            link(dve, dve.tensor_scalar(scrap[:, 0:T * H1].rearrange("p (t h) -> p t h", t=T), f.den[:, :, :], DEN_MAX,
                                        0.0, ALU.is_le, ALU.add, accum_out=f.full[:, 1:2]))
            link(dve, dve.reduce_sum(f.full_sum[:, :], f.full[:, 0:7], AX_X))
            assert at[0] == LINKS
            dve.wait_ge(tallied, 1)
            every = float(P * T * (H0 + H1 + NSEG + 4) + P * T // 2)
            dve.tensor_scalar(f.flag[0:1, 0:1], m.psum[0][0:1, 0:1], every, None, ALU.not_equal).then_inc(flagged, 1)
            dve.wait_ge(flagged, 1)

        @block.tensor
        def _(pe):
            pe.wait_ge(chain, LINKS)
            pe.matmul(m.psum[0][0:1, 0:1], f.full_sum[:, :], m.ones[:, 0:1], start=True, stop=True).then_inc(tallied, 1)

    return check_edges, check_all


def diagonal_of(adj):
    return bass.AP(adj.tensor, adj.offset, [[N + 1, P], [P * (N + 1), T], [1, 1]])


def sparse_path(nc, ctx, m, f, x, adj, weights, out):
    x_loaded = [ctx.enter_context(nc.semaphore(f"x_loaded{g}")) for g in range(GROUPS)]
    a_loaded = [ctx.enter_context(nc.semaphore(f"a_loaded{u}")) for u in range(2)]
    with nc.Block() as block:
        load_x(m, block, x, x_loaded)
        var_done = statistics(nc, ctx, m, block, x_loaded, "_0")
        prepare(nc, ctx, m, block, *weights)
        @block.scalar
        def _(act):
            for u in range(2):
                act.dma_start(f.adj[:, u, :], adj[u * P:(u + 1) * P, :]).then_inc(a_loaded[u], 16)
            act.dma_start(f.diagonal[:, :, None], diagonal_of(adj), allow_slow_non_contiguous=True
                          ).then_inc(f.diagonal_loaded, 16)

        sparse_constants(nc, ctx, m, f, block)
        root_done = take_roots(nc, ctx, m, block, "_0", var_done)
        sign_first(f, block, a_loaded)
        stored = transform(nc, ctx, m, block, 0, "_0", root_done)
        sent, parts_done = publish(nc, ctx, m, f, block, 0, stored)
        own_done = own_edges(nc, ctx, m, f, block, stored)
        finish = finish0(nc, ctx, m, f)
        find_and_attend0(nc, ctx, m, f, block, adj, a_loaded, stored, sent, parts_done, own_done, finish)
    with nc.Block() as block:
        root_done = take_roots(nc, ctx, m, block, "_1", finish.var_done)
        stored = transform(nc, ctx, m, block, 1, "_1", root_done)
        sent, parts_done = publish(nc, ctx, m, f, block, 1, stored)
        check_edges, check_all = checks(nc, ctx, m, f)
        x_done = attend1(nc, ctx, m, f, block, sent, parts_done, out, check_edges)
        check_all(block, x_done)


def any_path(nc, ctx, m, f, x, adj, out):
    def sb(name, shape, dt=F32):
        return ctx.enter_context(nc.sbuf_tensor(name, shape, dt))

    g = Memory()
    g.adj = f.adj[:, 0, :]
    g.e = f.adj[:, 1, :]
    g.row = f.adj[:, 2, :]
    g.att = f.sums[:, 0:T * D].rearrange("p (t d) -> p t d", t=T)
    own = f.own[:, :, :].rearrange("p t v -> p (t v)")
    g.diag = own[:, 0:BPC * P].rearrange("p (b q) -> p b q", b=BPC)
    g.p_t = own[:, BPC * P:BPC * P + 2 * CHUNK].rearrange("p (b q) -> p b q", b=2)
    g.top = sb("any_top", [P, 4])
    x_loaded = [ctx.enter_context(nc.semaphore("x_loaded_any"))]
    for layer in range(2):
        with nc.Block() as block:
            if layer == 0:
                load_x(m, block, x, x_loaded)
            var_done = statistics(nc, ctx, m, block, x_loaded, f"_any{layer}")
            root_done = take_roots(nc, ctx, m, block, f"_any{layer}", var_done)
            transform(nc, ctx, m, block, layer, f"_nodes{layer}", root_done)
        attend_any(nc, ctx, m, layer, adj, g, f"_any{layer}")
        finish_any(nc, ctx, m, layer, out, g, f"_end{layer}")


def build(nc, x, adj, W0, al, ar, W1, b1, a1, out):
    with ExitStack() as ctx:
        m = allocate(nc, ctx)
        f = allocate_sparse(nc, ctx)
        sparse_path(nc, ctx, m, f, x, adj, (W0, al, ar, W1, b1, a1), out)
        failed = nc.values_load(f.flag[0:1, 0:1], min_val=0, max_val=1, skip_runtime_bounds_check_because="0 or 1")
        with nc.If(failed > 0):
            nc.all_engine_barrier()
            any_path(nc, ctx, m, f, x, adj, out)


_INS = ['x', 'adj', 'L0_gnn_W', 'L0_gnn_a_l', 'L0_gnn_a_r', 'L1_gnn_W', 'L1_gnn_b', 'L1_gnn_a']
_OUTS = [((4096, 128), 'float32')]


def kernel(**inputs):
    import numpy as _np
    import concourse.bacc as _bacc
    from concourse import mybir as _mybir
    from concourse.bass_utils import run_bass_kernel_spmd as _run
    nc = _bacc.Bacc("TRN2", target_bir_lowering=False, num_devices=1)
    arrays, args = {}, []
    for name in _INS:
        a = _np.ascontiguousarray(inputs[name])
        arrays[f"in_{name}_dram"] = a
        args.append(nc.dram_tensor(f"in_{name}_dram", a.shape, _mybir.dt.from_np(a.dtype), kind="ExternalInput").ap())
    for i, (shape, dtype) in enumerate(_OUTS):
        dt = _mybir.dt.from_np(_np.dtype(dtype))
        args.append(nc.dram_tensor(f"out_{i}_dram", shape, dt, kind="ExternalOutput").ap())
    build(nc, *args)
    r = _run(nc, [arrays], core_ids=[0])
    return r.results[0]["out_0_dram"]
```
